# Optimizing a Trainium2 kernel written in Bass

```python
import numpy as np
import jax
import jax.numpy as jnp

def _softmax(x, axis=-1):
    return jax.nn.softmax(x, axis=axis)

def _gelu(x):
    return jax.nn.gelu(x, approximate=True)

def _silu(x):
    return jax.nn.silu(x)

def _sigmoid(x):
    return jax.nn.sigmoid(x)

def _layernorm(x, axis=-1, eps=1e-05):
    m = jnp.mean(x, axis=axis, keepdims=True)
    v = jnp.var(x, axis=axis, keepdims=True)
    return (x - m) / jnp.sqrt(v + eps)

def _scatter_add(tgt, idx, src, axis=0):
    return tgt.at[idx].add(src)

def _segment_sum(src, seg, n):
    return jax.ops.segment_sum(src, seg, n)
kernel_name = 'mk_gnn_resnorm_d2_gnn_r32_44449a'

def setup_inputs(seed: int=0):
    np.random.seed(seed)
    _w = jnp.asarray

    def _rec_inputs():
        import jax
        import jax.numpy as jnp
        _gk = jax.random.key(seed)
        x = -0.0001006 + 1 * jax.random.normal(jax.random.fold_in(_gk, 1), (50000, 96), jnp.float32)
        src = jax.random.randint(jax.random.fold_in(_gk, 2), (25000,), 0, 50000, jnp.int32)
        dst = jax.random.randint(jax.random.fold_in(_gk, 3), (25000,), 0, 50000, jnp.int32)
        _o = jnp.argsort(dst, stable=True)
        src = src[_o]
        dst = dst[_o]
        edge_attr_32 = 0.000196303 + 1.00016 * jax.random.normal(jax.random.fold_in(_gk, 12), (25000, 32), jnp.float32)
        return (x, src, dst, edge_attr_32)
    x, src, dst, edge_attr_32 = _rec_inputs()

    def _L0_gnn_setup():
        import jax, jax.numpy as jnp
        import numpy as np
        N, E = (50000, 25000)
        DIN = DOUT = 96
        DE = 32

        def _egnn_conv(x, src, dst, edge_attr, W_msg, W_edge, W_root, b):
            msg = x[src] @ W_msg + edge_attr @ W_edge
            agg = jax.ops.segment_max(msg, dst, num_segments=x.shape[0])
            agg = jnp.where(jnp.isneginf(agg), 0.0, agg)
            return agg + x @ W_root + b
        key = jax.random.key(seed)
        ks = jax.random.split(key, 10)
        rn = lambda k, sh, sc: jax.random.normal(k, sh, jnp.float32) * sc
        return {'X': rn(ks[0], (N, DIN), 1.0), 'edge_index': jax.random.randint(ks[1], (2, E), 0, N, jnp.int32), 'edge_attr': rn(ks[2], (E, DE), 1.0), 'W1_msg': rn(ks[3], (DIN, DOUT), DIN ** (-0.5)), 'W1_edge': rn(ks[4], (DE, DOUT), DE ** (-0.5)), 'W1_root': rn(ks[5], (DIN, DOUT), DIN ** (-0.5)), 'b1': jnp.zeros((DOUT,), jnp.float32), 'W2_msg': rn(ks[6], (DOUT, DOUT), DOUT ** (-0.5)), 'W2_edge': rn(ks[7], (DE, DOUT), DE ** (-0.5)), 'W2_root': rn(ks[8], (DOUT, DOUT), DOUT ** (-0.5)), 'b2': jnp.zeros((DOUT,), jnp.float32)}
    _L0_gnn_all = _L0_gnn_setup()
    _L0_gnn_in = {k: v for k, v in _L0_gnn_all.items() if k in ('W1_msg', 'W1_edge', 'W1_root', 'b1', 'W2_msg', 'W2_edge', 'W2_root', 'b2')}
    del _L0_gnn_all

    def _L1_gnn_setup():
        import jax, jax.numpy as jnp
        import numpy as np
        N_NODES = 50000
        N_EDGES = 25000
        D_MODEL = 96
        HEADS = 4
        key = jax.random.key(seed)
        ks = jax.random.split(key, 6)
        scale = 1.0 / np.sqrt(D_MODEL)
        return {'embeds': jax.random.normal(ks[0], (N_NODES, D_MODEL), dtype=jnp.float32), 'qW': jax.random.normal(ks[1], (D_MODEL, D_MODEL), dtype=jnp.float32) * scale, 'kW': jax.random.normal(ks[2], (D_MODEL, D_MODEL), dtype=jnp.float32) * scale, 'vW': jax.random.normal(ks[3], (D_MODEL, D_MODEL), dtype=jnp.float32) * scale, 'rows': jax.random.randint(ks[4], (N_EDGES,), 0, N_NODES, dtype=jnp.int32), 'cols': jax.random.randint(ks[5], (N_EDGES,), 0, N_NODES, dtype=jnp.int32)}
    _L1_gnn_all = _L1_gnn_setup()
    _L1_gnn_in = {k: v for k, v in _L1_gnn_all.items() if k in ('qW', 'kW', 'vW')}
    del _L1_gnn_all
    return {'x': x, 'src': src, 'dst': dst, 'edge_attr_32': edge_attr_32, 'L0_gnn_W1_msg': _L0_gnn_in['W1_msg'], 'L0_gnn_W1_edge': _L0_gnn_in['W1_edge'], 'L0_gnn_W1_root': _L0_gnn_in['W1_root'], 'L0_gnn_b1': _L0_gnn_in['b1'], 'L0_gnn_W2_msg': _L0_gnn_in['W2_msg'], 'L0_gnn_W2_edge': _L0_gnn_in['W2_edge'], 'L0_gnn_W2_root': _L0_gnn_in['W2_root'], 'L0_gnn_b2': _L0_gnn_in['b2'], 'L1_gnn_qW': _L1_gnn_in['qW'], 'L1_gnn_kW': _L1_gnn_in['kW'], 'L1_gnn_vW': _L1_gnn_in['vW']}

def reference(x, src, dst, edge_attr_32, L0_gnn_W1_msg, L0_gnn_W1_edge, L0_gnn_W1_root, L0_gnn_b1, L0_gnn_W2_msg, L0_gnn_W2_edge, L0_gnn_W2_root, L0_gnn_b2, L1_gnn_qW, L1_gnn_kW, L1_gnn_vW):
    import jax
    import jax.numpy as jnp

    def _L0_gnn_ref(X, edge_index, edge_attr, W1_msg, W1_edge, W1_root, b1, W2_msg, W2_edge, W2_root, b2):
        import jax, jax.numpy as jnp
        import numpy as np
        N, E = (50000, 25000)
        DIN = DOUT = 96
        DE = 32

        def _egnn_conv(x, src, dst, edge_attr, W_msg, W_edge, W_root, b):
            msg = x[src] @ W_msg + edge_attr @ W_edge
            agg = jax.ops.segment_max(msg, dst, num_segments=x.shape[0])
            agg = jnp.where(jnp.isneginf(agg), 0.0, agg)
            return agg + x @ W_root + b
        src, dst = (edge_index[0], edge_index[1])
        c1 = jax.nn.leaky_relu(_egnn_conv(X, src, dst, edge_attr, W1_msg, W1_edge, W1_root, b1))
        c2 = jax.nn.leaky_relu(_egnn_conv(c1, src, dst, edge_attr, W2_msg, W2_edge, W2_root, b2))
        return c2

    def _L1_gnn_ref(embeds, qW, kW, vW, rows, cols):
        import jax, jax.numpy as jnp
        import numpy as np
        N_NODES = 50000
        N_EDGES = 25000
        D_MODEL = 96
        HEADS = 4
        nvar, d = embeds.shape
        dh = d // HEADS
        e = rows.shape[0]
        q = (embeds[rows] @ qW).reshape(e, HEADS, dh)
        k = (embeds[cols] @ kW).reshape(e, HEADS, dh)
        v = (embeds[cols] @ vW).reshape(e, HEADS, dh)
        scores = jnp.clip(jnp.einsum('ehd,ehd->eh', q, k), -10.0, 10.0)
        exp_s = jnp.exp(scores)
        norms = jax.ops.segment_sum(exp_s, rows, num_segments=nvar)[rows]
        w = exp_s / (norms + 1e-08)
        res = jax.ops.segment_sum(w[:, :, None] * v, rows, num_segments=nvar).reshape(nvar, d)
        return embeds + res
    edge_index = jnp.stack([src, dst])
    x = _layernorm(x + _L0_gnn_ref(x, edge_index, edge_attr_32, L0_gnn_W1_msg, L0_gnn_W1_edge, L0_gnn_W1_root, L0_gnn_b1, L0_gnn_W2_msg, L0_gnn_W2_edge, L0_gnn_W2_root, L0_gnn_b2), axis=-1)
    x = _layernorm(x + _L1_gnn_ref(x, L1_gnn_qW, L1_gnn_kW, L1_gnn_vW, src, dst), axis=-1)
    return x

_drawn_inputs = setup_inputs


def setup_inputs(seed=0):
    import zlib

    import numpy as np

    out = dict(_drawn_inputs(seed))
    spreads = {'L0_gnn_b1': (0.0, 0.1), 'L0_gnn_b2': (0.0, 0.1)}
    factors = {}
    for name, (base, spread) in spreads.items():
        noise = np.random.default_rng([zlib.crc32(name.encode()), seed]).standard_normal(out[name].shape)
        drawn = base * np.exp(spread * noise) if base else spread * noise
        out[name] = jnp.asarray(drawn.astype(out[name].dtype))
    for name, factor in factors.items():
        out[name] = (out[name] * factor).astype(out[name].dtype)
    return out
```

```python
import concourse.bass as bass
from concourse import mybir
from contextlib import ExitStack

F32 = mybir.dt.float32
I32 = mybir.dt.int32
ALU = mybir.AluOpType
ACT = mybir.ActivationFunctionType
AX = mybir.AxisListType


def gnn_program(nc, x, edge_attr, src_tiles, dst_tiles, dst_next_tiles, src_line, dst_line,
                w_msg, w_edge, w_root, bias, w_q, w_k, w_v, out):
    N, D = x.shape
    E, DE = edge_attr.shape
    P = 125
    TILES = E // P
    TG = 4
    GROUPS = TILES // TG
    GE = TG * P
    ROWS = N // (GROUPS * P)
    HALF = ROWS // 2
    BLOCK = P * ROWS
    HEADS = 4
    DH = D // HEADS
    DV = D + HEADS
    SLOTS = 2 * TG
    SPARE = SLOTS * P
    SPLIT = 80
    SLOPE = 0.01
    EPS = 1e-5
    NEG = -3.0e38
    STEP = 3.0e33
    assert TILES * P == E and GROUPS * TG == TILES and BLOCK * GROUPS == N and GROUPS % 2 == 0
    assert HEADS * DH == D and D + DE == 128

    y1_table = nc.dram_tensor("y1_table", (N + SPARE, D), F32, kind="Internal").ap()
    z2x_table = nc.dram_tensor("z2x_table", (N + SPARE, 2 * D), F32, kind="Internal").ap()
    z2_rows = z2x_table.rearrange("n (two d) -> (n two) d", two=2)
    sum_table = nc.dram_tensor("sum_table", (N + SPARE, DV), F32, kind="Internal").ap()

    ctx = ExitStack()
    with ctx:
        def sb(name, shape, dt=F32):
            return ctx.enter_context(nc.sbuf_tensor(name, shape, dt))

        def sem(name):
            return ctx.enter_context(nc.semaphore(name))

        bank = [ctx.enter_context(nc.psum_tensor(f"bank{i}", [128, 512], F32)) for i in range(8)]

        ident = sb("ident", [128, 128])
        wcat = [sb(f"wcat{i}", [128, D]) for i in range(2)]
        wroot = [sb(f"wroot{i}", [D, D]) for i in range(2)]
        bias_b = [sb(f"bias_b{i}", [P, D]) for i in range(2)]
        wq = sb("wq", [D, D])
        wkv = sb("wkv", [D, 2 * D])
        src_i = sb("src_i", [P, TILES + SLOTS], I32)
        dst_i = sb("dst_i", [P, TILES + SLOTS], I32)
        next_i = sb("next_i", [P, TILES], I32)
        src_f = sb("src_f", [P, TILES])
        dst_f = sb("dst_f", [P, TILES])
        next_f = sb("next_f", [P, TILES])
        spare_i = sb("spare_i", [P, TILES], I32)
        spare_f = sb("spare_f", [P, TILES])
        put = [sb(f"put{i}", [P, TILES], I32) for i in range(3)]
        put_f = sb("put_f", [P, TILES])
        earlier_count = sb("earlier_count", [P, TILES])
        earlier = sb("earlier", [P, TG, GE])
        zeros = sb("zeros", [P, ROWS, DV])
        eps = sb("eps", [P, 2, ROWS])
        rows_all = sb("rows_all", [P, TILES, D])

        take_idx = sb("take_idx", [P, SLOTS], I32)
        take_dst = sb("take_dst", [P, SLOTS], I32)
        put_idx = sb("put_idx", [P, SLOTS], I32)
        gath = sb("gath", [P, 2, TG, D + DE])
        put_rows = sb("put_rows", [P, 2, TG, D])
        featT = sb("featT", [128, 2, GE])
        msg_max = sb("msg_max", [D, 2, GE])
        dst_row = sb("dst_row", [D, 2, GE + 1], I32)
        dst_scaled = sb("dst_scaled", [D, 2, GE + 1])
        cut = sb("cut", [D, 2, GE])
        src_row = sb("src_row", [P, 2, GE], I32)
        same = sb("same", [P, TG, GE])
        node_in = sb("node_in", [P, 2, ROWS, D])
        nodeT = sb("nodeT", [D, 2, HALF * P])
        y_out = sb("y_out", [P, 2, ROWS, D])
        zx_out = sb("zx_out", [P, 2, ROWS, 2 * D])

        loaded = sem("loaded")
        zero_set = sem("zero_set")
        spare_set = sem("spare_set")
        sums_zeroed = sem("sums_zeroed")
        consts_made = sem("consts_made")
        index_step = sem("index_step")
        puts_made = sem("puts_made")
        sp_turns = sem("sp_turns")
        pool_turns = sem("pool_turns")

        class Step:

            def __init__(self, eng, base, u, kept):
                self.eng, self.base, self.u, self.kept = eng, base, u, kept

            def at(self, k):
                if isinstance(self.base, int):
                    return self.base + self.u + k
                n = self.u + k
                if n not in self.kept:
                    self.kept[n] = self.eng.snap(self.base + n)
                return self.kept[n]

            def times(self, k, m):
                if isinstance(self.base, int):
                    return (self.base // 2 + k) * m
                key = ("x", k, m)
                if key not in self.kept:
                    self.kept[key] = self.eng.snap(self.base // 2 * m + k * m)
                return self.kept[key]

            def scaled(self, m):
                if isinstance(self.base, int):
                    return (self.base + self.u) * m
                key = ("s", self.u, m)
                if key not in self.kept:
                    self.kept[key] = self.eng.snap(self.base * m + self.u * m)
                return self.kept[key]

        def wait(eng, s, value):
            if isinstance(value, int) and value <= 0:
                return
            eng.wait_ge(s, value)

        def steps(eng, body, first=0, last=GROUPS):
            for u in range(2):
                body(Step(eng, first, u, {}))
            with eng.Fori(first // 2 + 1, last // 2) as t:
                base = eng.snap(t * 2)
                kept = {}
                for u in range(2):
                    body(Step(eng, base, u, kept))

        def pair(name):
            return [sem(f"{name}_{u}") for u in range(2)]

        class Layer:
            def __init__(self, n):
                self.n = n
                self.idx_staged = sem(f"layer{n}_idx_staged")
                self.feat_taken = sem(f"layer{n}_feat_taken")
                self.featT_copied = sem(f"layer{n}_featT_copied")
                self.cut_scaled = sem(f"layer{n}_cut_scaled")
                self.cut_made = sem(f"layer{n}_cut_made")
                self.msg_done = sem(f"layer{n}_msg_done")
                self.max_done = sem(f"layer{n}_max_done")
                self.back_done = sem(f"layer{n}_back_done")
                self.rows_kept = sem(f"layer{n}_rows_kept")
                self.gath_ready = sem(f"layer{n}_gath_ready")
                self.node_ready = sem(f"layer{n}_node_ready")
                self.put_staged = sem(f"layer{n}_put_staged")
                self.sames_counted = sem(f"layer{n}_sames_counted")
                self.node_taken = pair(f"layer{n}_node_taken")
                self.nodeT_copied = pair(f"layer{n}_nodeT_copied")
                self.root_done = pair(f"layer{n}_root_done")
                self.y_made = pair(f"layer{n}_y_made")
                self.gathered = pair(f"layer{n}_gathered")
                self.attr_in = pair(f"layer{n}_attr_in")
                self.rows_in = pair(f"layer{n}_rows_in")
                self.nodes_in = pair(f"layer{n}_nodes_in")
                self.y_stored = pair(f"layer{n}_y_stored")
                self.put_done = pair(f"layer{n}_put_done")

        class Attention:
            def __init__(self):
                self.idx_staged = sem("att_idx_staged")
                self.taken = sem("att_taken")
                self.var_made = sem("att_var_made")
                self.rstd_made = sem("att_rstd_made")
                self.shift_made = sem("att_shift_made")
                self.x1_made = sem("att_x1_made")
                self.x1T_done = sem("att_x1T_done")
                self.x1T_copied = sem("att_x1T_copied")
                self.qkv_done = sem("att_qkv_done")
                self.q_copied = sem("att_q_copied")
                self.prod_made = sem("att_prod_made")
                self.score_made = sem("att_score_made")
                self.clip_made = sem("att_clip_made")
                self.exp_made = sem("att_exp_made")
                self.val_made = sem("att_val_made")
                self.same_made = sem("att_same_made")
                self.sums_done = sem("att_sums_done")
                self.sums_staged = sem("att_sums_staged")
                self.leaky_made = sem("att_leaky_made")
                self.moments_made = sem("att_moments_made")
                self.gathered = pair(f"att_gathered")
                self.rows_in = pair(f"att_rows_in")
                self.put_done = pair(f"att_put_done")
                self.stats_made = pair(f"att_stats_made")

        class LastPass:
            def __init__(self):
                self.leaky_made = sem("last_leaky_made")
                self.pre_made = sem("last_pre_made")
                self.moments_made = sem("last_moments_made")
                self.var_made = sem("last_var_made")
                self.rstd_made = sem("last_rstd_made")
                self.x1_made = sem("last_x1_made")
                self.shift_made = sem("last_shift_made")
                self.norm_made = sem("last_norm_made")
                self.inv_made = sem("last_inv_made")
                self.res_made = sem("last_res_made")
                self.sum_made = sem("last_sum_made")
                self.moments2_made = sem("last_moments2_made")
                self.var2_made = sem("last_var2_made")
                self.rstd2_made = sem("last_rstd2_made")
                self.shift2_made = sem("last_shift2_made")
                self.out_made = sem("last_out_made")
                self.blocks_in = pair(f"last_blocks_in")
                self.stored = pair(f"last_stored")
                self.stats_made = pair(f"last_stats_made")
                self.stats2_made = pair(f"last_stats2_made")

        layers = [Layer(0), Layer(1)]
        att = Attention()
        fin = LastPass()
        GATHERED = 16 * TG

        pool_bytes = rows_all[:, :, :].rearrange("p t d -> p (t d)")
        taken_at = [0]

        def carve(*shape):
            size = 1
            for s in shape:
                size *= s
            at = taken_at[0]
            taken_at[0] += size
            assert taken_at[0] <= TILES * D
            v = pool_bytes[:, at:at + size]
            if len(shape) == 2:
                return v.rearrange("p (a b) -> p a b", b=shape[1])
            return v.rearrange("p (a b c) -> p a b c", b=shape[1], c=shape[2])

        g_both = carve(2, 2 * TG, 2 * D)
        pre = carve(2, 2 * TG, D)
        x1 = carve(2, 2 * TG, D)
        moments = carve(2, 2 * TG, 6)
        apart = carve(1, 2 * TG)[:, 0, :]
        squares = carve(1, 2 * TG)[:, 0, :]
        mean2 = carve(2, 2 * TG)
        rstd = carve(2, 2 * TG)
        shift = carve(2, 2 * TG)
        var_eps = carve(2, 2 * TG)
        q_sb = carve(TG, D)
        prod = carve(TG, D)
        scores = carve(TG, HEADS)
        clipped = carve(TG, HEADS)
        vals = carve(2, TG, DV)
        sums = carve(2, TG, DV)
        x1T = sb("x1T", [D, 2, GE])
        half_pow = sb("half_pow", [P, 2 * TG])

        fin_sums = sb("fin_sums", [P, 2, ROWS, DV])
        rstd2 = sb("rstd2", [P, 2, ROWS])
        shift2 = sb("shift2", [P, 2, ROWS])
        var_eps2 = sb("var_eps2", [P, 2, ROWS])
        moments2 = sb("moments2", [P, 2, ROWS, 6])
        den = sb("den", [P, ROWS, HEADS])
        inv_den = sb("inv_den", [P, ROWS, HEADS])

        block = ctx.enter_context(nc.Block())

        def node_block(table, row):
            v = table[bass.ds(row, BLOCK), :].rearrange("(p r) d -> p r d", r=ROWS)
            return [(v[a:b], a, b) for a, b in ((0, SPLIT), (SPLIT, P))]

        NODE_DMAS = 32

        @block.sync
        def _(sp):
            loads = [(wq[:, :], w_q), (wkv[:, 0:D], w_k), (wkv[:, D:2 * D], w_v),
                     (src_i[:, 0:TILES], src_tiles), (dst_i[:, 0:TILES], dst_tiles), (next_i[:, :], dst_next_tiles)]
            for n in range(2):
                loads += [(wcat[n][0:D, :], w_msg[n]), (wcat[n][D:D + DE, :], w_edge[n]), (wroot[n][:, :], w_root[n]),
                          (bias_b[n][:, :], bias[n][None, :].to_broadcast([P, D]))]
            for to, of in loads:
                sp.dma_start(to, of).then_inc(loaded, 16)

            sp.wait_ge(zero_set, 1)
            sp.dma_start(y1_table[N:N + SPARE, :].rearrange("(p r) d -> p r d", r=SLOTS),
                         zeros[:, :, 0:D]).then_inc(spare_set, 16)
            for h in range(2):
                sp.dma_start(z2x_table[N:N + SPARE, h * D:(h + 1) * D].rearrange("(p r) d -> p r d", r=SLOTS),
                             zeros[:, :, 0:D]).then_inc(spare_set, 16)
            sp.dma_start(sum_table[N:N + SPARE, :].rearrange("(p r) d -> p r d", r=SLOTS),
                         zeros[:, :, :]).then_inc(spare_set, 16)

            for L in layers:
                n = L.n

                def load(s, L=L, n=n):
                    edge, node, u = s.scaled(GE), s.scaled(BLOCK), s.u
                    wait(sp, L.feat_taken, s.at(-1))
                    sp.dma_start(gath[:, u, :, D:D + DE],
                                 edge_attr[bass.ds(edge, GE), :].rearrange("(j p) d -> p j d", p=P)
                                 ).then_inc(L.attr_in[u], 16)
                    wait(sp, L.cut_scaled, s.at(-1))
                    sp.sem_inc(sp_turns, 1)
                    sp.dma_start(dst_row[:, u, :], dst_line[bass.ds(edge, GE + 1)][None, :].to_broadcast([D, GE + 1])
                                 ).then_inc(L.rows_in[u], 16)
                    if n == 0:
                        wait(sp, L.sames_counted, s.at(-1))
                        sp.dma_start(src_row[:, u, :], src_line[bass.ds(edge, GE)][None, :].to_broadcast([P, GE])
                                     ).then_inc(L.rows_in[u], 16)
                    wait(sp, L.node_taken[1], s.at(-1))
                    for v, a, b in node_block(x if n == 0 else y1_table, node):
                        sp.dma_start(node_in[a:b, u], v).then_inc(L.nodes_in[u], 16)
                    if n == 1:
                        wait(sp, L.y_stored[u], s.times(0, NODE_DMAS))
                        for v, a, b in node_block(x, node):
                            sp.dma_start(zx_out[a:b, u, :, D:2 * D], v).then_inc(L.nodes_in[u], 16)
                    if n == 0:
                        for v, a, b in node_block(sum_table, node):
                            sp.dma_start(v, zeros[a:b]).then_inc(sums_zeroed, 16)

                def store(s, L=L, n=n):
                    node, u = s.scaled(BLOCK), s.u
                    wait(sp, L.y_made[1], s.at(1))
                    for v, a, b in node_block(y1_table if n == 0 else z2x_table, node):
                        sp.dma_start(v, (y_out if n == 0 else zx_out)[a:b, u]).then_inc(L.y_stored[u], 16)

                if n == 1:
                    for u in range(2):
                        sp.wait_ge(layers[0].put_done[u], 16 * TG * GROUPS // 2)
                load(Step(sp, 0, 0, {}))
                load(Step(sp, 0, 1, {}))
                with sp.Fori(1, GROUPS // 2) as t:
                    before = sp.snap(t * 2 - 2)
                    base = sp.snap(t * 2)
                    k0, k1 = {}, {}
                    for u in range(2):
                        store(Step(sp, before, u, k0))
                        load(Step(sp, base, u, k1))
                for u in range(2):
                    store(Step(sp, GROUPS - 2, u, {}))

            def load_att(s):
                edge = s.scaled(GE)
                wait(sp, att.same_made, s.at(-1))
                sp.dma_start(src_row[:, s.u, :], src_line[bass.ds(edge, GE)][None, :].to_broadcast([P, GE])
                             ).then_inc(att.rows_in[s.u], 16)

            sp.wait_ge(layers[0].sames_counted, GROUPS)
            steps(sp, load_att)

            for u in range(2):
                sp.wait_ge(att.put_done[u], 16 * TG * GROUPS // 2)

            def load_fin(s):
                node, u = s.scaled(BLOCK), s.u
                wait(sp, fin.pre_made, s.at(-1))
                for v, a, b in node_block(z2x_table, node):
                    sp.dma_start(zx_out[a:b, u], v).then_inc(fin.blocks_in[u], 16)
                wait(sp, fin.res_made, s.at(-1))
                for v, a, b in node_block(sum_table, node):
                    sp.dma_start(fin_sums[a:b, u], v).then_inc(fin.blocks_in[u], 16)

            def store_fin(s):
                node = s.scaled(BLOCK)
                wait(sp, fin.out_made, s.at(1))
                for v, a, b in node_block(out, node):
                    sp.dma_start(v, y_out[a:b, s.u]).then_inc(fin.stored[s.u], 16)

            load_fin(Step(sp, 0, 0, {}))
            load_fin(Step(sp, 0, 1, {}))
            with sp.Fori(1, GROUPS // 2) as t:
                before = sp.snap(t * 2 - 2)
                base = sp.snap(t * 2)
                k0, k1 = {}, {}
                for u in range(2):
                    store_fin(Step(sp, before, u, k0))
                    load_fin(Step(sp, base, u, k1))
            for u in range(2):
                store_fin(Step(sp, GROUPS - 2, u, {}))
            for u in range(2):
                sp.wait_ge(fin.stored[u], NODE_DMAS * GROUPS // 2)

        @block.gpsimd
        def _(pool):
            nc.gpsimd.memset(zeros[:], 0.0).then_inc(zero_set, 1)
            nc.gpsimd.memset(ident[:], 0.0).then_inc(consts_made, 1)
            nc.gpsimd.memset(earlier[:], 1.0).then_inc(consts_made, 1)
            nc.gpsimd.memset(half_pow[:], -0.5).then_inc(consts_made, 1)
            nc.gpsimd.memset(src_i[:, TILES:], 0)
            nc.gpsimd.memset(dst_i[:, TILES:], 0)
            nc.gpsimd.iota(spare_i[:, :].rearrange("p (a b) -> p a b", b=SLOTS), pattern=[[0, TILES // SLOTS], [P, SLOTS]], base=N,
                           channel_multiplier=1).then_inc(consts_made, 1)
            pool.wait_ge(consts_made, 4)
            nc.gpsimd.affine_select(out=ident[:], in_=ident[:], compare_op=ALU.not_equal, fill=1.0, base=0,
                                    pattern=[[-1, 128]], channel_multiplier=1).then_inc(consts_made, 1)
            nc.gpsimd.affine_select(out=earlier[:], in_=earlier[:], compare_op=ALU.is_gt, fill=0.0, base=0,
                                    pattern=[[P, TG], [-1, GE]], channel_multiplier=1).then_inc(consts_made, 1)

            for L in layers:
                table = x if L.n == 0 else y1_table
                if L.n == 1:
                    for u in range(2):
                        pool.wait_ge(layers[0].put_done[u], 16 * TG * GROUPS // 2)

                def gather(s, L=L, table=table):
                    u = s.u
                    wait(pool, L.feat_taken, s.at(-1))
                    wait(pool, L.idx_staged, s.at(1))
                    pool.sem_inc(pool_turns, 1)
                    for j in range(TG):
                        pool.indirect_dma_start(
                            out=gath[:, u, j, 0:D], out_offset=None, in_=table[0:N, :],
                            in_offset=bass.IndirectOffsetOnAxis(ap=take_idx[:, u * TG + j:u * TG + j + 1], axis=0),
                        ).then_inc(L.gathered[u], 16)

                steps(pool, gather)
                for u in range(2):
                    pool.wait_ge(L.y_stored[u], NODE_DMAS * GROUPS // 2)
                pool.wait_ge(spare_set, 64)
                rows = y1_table if L.n == 0 else z2_rows

                def scatter(s, L=L, rows=rows):
                    u = s.u
                    wait(pool, L.put_staged, s.at(1))
                    pool.sem_inc(pool_turns, 1)
                    for j in range(TG):
                        pool.indirect_dma_start(
                            out=rows, in_=put_rows[:, u, j, :], in_offset=None,
                            out_offset=bass.IndirectOffsetOnAxis(ap=put_idx[:, u * TG + j:u * TG + j + 1], axis=0),
                            compute_op=ALU.add,
                        ).then_inc(L.put_done[u], 16)

                steps(pool, scatter)

            for u in range(2):
                pool.wait_ge(layers[1].put_done[u], 16 * TG * GROUPS // 2)
            pool.wait_ge(sums_zeroed, NODE_DMAS * GROUPS)

            def gather_both(s):
                u = s.u
                wait(pool, att.taken, s.at(-1))
                wait(pool, att.idx_staged, s.at(1))
                pool.sem_inc(pool_turns, 1)
                for j in range(2 * TG):
                    idx = take_idx if j < TG else take_dst
                    c = u * TG + j % TG
                    pool.indirect_dma_start(
                        out=g_both[:, u, j, :], out_offset=None, in_=z2x_table[0:N, :],
                        in_offset=bass.IndirectOffsetOnAxis(ap=idx[:, c:c + 1], axis=0),
                    ).then_inc(att.gathered[u], 16)

            def inv_std(s):
                wait(pool, att.var_made, s.at(1))
                wait(pool, att.x1_made, s.at(-1))
                nc.gpsimd.tensor_tensor(rstd[:, s.u, :], var_eps[:, s.u, :], half_pow[:, :],
                                        ALU.pow).then_inc(att.rstd_made, 1)

            def scatter_sums(s, before):
                u = s.u
                if before is not None:
                    wait(pool, att.put_done[1 - u], before)
                wait(pool, att.sums_staged, s.at(1))
                pool.sem_inc(pool_turns, 1)
                for j in range(TG):
                    pool.indirect_dma_start(
                        out=sum_table, in_=sums[:, u, j, :], in_offset=None,
                        out_offset=bass.IndirectOffsetOnAxis(ap=put_idx[:, u * TG + j:u * TG + j + 1], axis=0),
                        compute_op=ALU.add,
                    ).then_inc(att.put_done[u], 16)

            PUTS = 16 * TG
            for u in range(2):
                gather_both(Step(pool, 0, u, {}))
                inv_std(Step(pool, 0, u, {}))
            gather_both(Step(pool, 2, 0, {}))
            scatter_sums(Step(pool, 0, 0, {}), None)
            inv_std(Step(pool, 2, 0, {}))
            gather_both(Step(pool, 2, 1, {}))
            scatter_sums(Step(pool, 0, 1, {}), PUTS)
            inv_std(Step(pool, 2, 1, {}))
            with pool.Fori(2, GROUPS // 2) as t:
                before = pool.snap(t * 2 - 2)
                base = pool.snap(t * 2)
                k0, k1 = {}, {}
                for u in range(2):
                    s0, s1 = Step(pool, before, u, k0), Step(pool, base, u, k1)
                    gather_both(s1)
                    scatter_sums(s0, s0.times(u, PUTS))
                    inv_std(s1)
            for u in range(2):
                s0 = Step(pool, GROUPS - 2, u, {})
                scatter_sums(s0, s0.times(u, PUTS))

            def inv_std_fin(which):
                def f(s):
                    a, b, c = ((fin.var_made, fin.rstd_made, fin.shift_made), (fin.var2_made, fin.rstd2_made, fin.shift2_made))[which]
                    wait(pool, a, s.at(1))
                    wait(pool, c, s.at(-1))
                    dst = rstd if which == 0 else rstd2
                    nc.gpsimd.tensor_tensor(dst[:, s.u, :], (var_eps if which == 0 else var_eps2)[:, s.u, :], half_pow[:, :],
                                            ALU.pow).then_inc(b, 1)
                return f

            def fin_both(s):
                inv_std_fin(0)(s)
                inv_std_fin(1)(s)

            steps(pool, fin_both)

        @block.scalar
        def _(act):
            act.wait_ge(loaded, 16 * 14)
            act.wait_ge(consts_made, 6)

            def stage_take(s_at, u, into, of, done):
                cp = nc.scalar.copy(into[:, u * TG:(u + 1) * TG], of[:, bass.ds(s_at * TG, TG)])
                if done is not None:
                    cp.then_inc(done, 1)

            for L in layers:
                n = L.n

                for u in range(2):
                    stage_take(u, u, take_idx, src_i, L.idx_staged)

                def body(s, L=L, n=n):
                    u = s.u
                    wait(act, L.rows_in[u], s.times(1, 32 if n == 0 else 16))
                    wait(act, L.cut_made, s.at(-1))
                    nc.scalar.activation(dst_scaled[:, u, :], dst_row[:, u, :], ACT.Copy,
                                         scale=STEP).then_inc(L.cut_scaled, 1)
                    wait(act, L.feat_taken, s.at(1))
                    wait(act, L.msg_done, s.at(-1))
                    nc.scalar.copy(featT[:, u, :], bank[u][:, 0:GE]).then_inc(L.featT_copied, 1)
                    stage_take(s.at(2), u, take_idx, src_i, L.idx_staged)
                    for h in range(2):
                        wait(act, L.node_taken[h], s.at(1))
                        wait(act, L.root_done[h], s.at(0))
                        nc.scalar.copy(nodeT[:, h, :], bank[4 + h][0:D, 0:HALF * P]).then_inc(L.nodeT_copied[h], 1)
                    wait(act, L.back_done, s.at(1))
                    nc.scalar.copy(rows_all[:, bass.ds(s.at(0) * TG, TG), :].rearrange("p t d -> p (t d)"),
                                   bank[3][0:P, 0:TG * D]).then_inc(L.rows_kept, 1)

                steps(act, body)

                act.wait_ge(puts_made, n + 1)
                act.wait_ge(L.rows_kept, GROUPS)

                def stage(s, L=L, n=n):
                    u = s.u
                    wait(act, L.put_done[u], s.times(0, 16 * TG))
                    nc.scalar.copy(put_idx[:, u * TG:(u + 1) * TG], put[n][:, bass.ds(s.at(0) * TG, TG)])
                    nc.scalar.copy(put_rows[:, u], rows_all[:, bass.ds(s.at(0) * TG, TG), :]).then_inc(L.put_staged, 1)

                steps(act, stage)

            act.wait_ge(puts_made, 3)
            for u in range(2):
                act.wait_ge(layers[1].put_done[u], 16 * TG * GROUPS // 2)
            for u in range(2):
                stage_take(u, u, take_idx, src_i, None)
                stage_take(u, u, take_dst, dst_i, att.idx_staged)

            def attend(s):
                u = s.u
                wait(act, att.gathered[u], s.times(1, 16 * 2 * TG))
                wait(act, att.taken, s.at(1))
                stage_take(s.at(2), u, take_idx, src_i, None)
                stage_take(s.at(2), u, take_dst, dst_i, att.idx_staged)
                wait(act, att.shift_made, s.at(1))
                wait(act, att.x1T_done, s.at(-1))
                for j in range(2 * TG):
                    last = nc.scalar.activation(x1[:, u, j, :], pre[:, u, j, :], ACT.Identity,
                                                scale=rstd[:, u, j:j + 1], bias=shift[:, u, j:j + 1])
                last.then_inc(att.x1_made, 1)
                wait(act, att.x1T_done, s.at(1))
                wait(act, att.qkv_done, s.at(0))
                nc.scalar.copy(x1T[:, 0, :], bank[0][0:D, 0:GE])
                nc.scalar.copy(x1T[:, 1, :], bank[1][0:D, 0:GE]).then_inc(att.x1T_copied, 1)
                wait(act, att.qkv_done, s.at(1))
                wait(act, att.prod_made, s.at(0))
                nc.scalar.copy(q_sb[:].rearrange("p j d -> p (j d)"), bank[2][0:P, 0:TG * D]).then_inc(att.q_copied, 1)
                wait(act, att.clip_made, s.at(1))
                wait(act, att.sums_done, s.at(-1))
                nc.scalar.activation(vals[:, u, :, D:DV], clipped[:], ACT.Exp).then_inc(att.exp_made, 1)
                wait(act, att.sums_done, s.at(1))
                wait(act, att.put_done[u], s.times(0, 16 * TG))
                nc.scalar.copy(put_idx[:, u * TG:(u + 1) * TG], put[2][:, bass.ds(s.at(0) * TG, TG)])
                nc.scalar.copy(sums[:, u].rearrange("p j d -> p (j d)"), bank[5][0:P, 0:TG * DV]).then_inc(att.sums_staged, 1)

            steps(act, attend)

            def finish(s):
                u = s.u
                wait(act, fin.shift_made, s.at(1))
                wait(act, fin.sum_made, s.at(-1))
                for r in range(ROWS):
                    last = nc.scalar.activation(x1[:, u, r, :], pre[:, u, r, :], ACT.Identity,
                                                scale=rstd[:, u, r:r + 1], bias=shift[:, u, r:r + 1])
                last.then_inc(fin.x1_made, 1)
                wait(act, fin.shift2_made, s.at(1))
                wait(act, fin.stored[u], s.times(0, NODE_DMAS))
                for r in range(ROWS):
                    last = nc.scalar.activation(y_out[:, u, r, :], x1[:, u, r, :], ACT.Identity,
                                                scale=rstd2[:, u, r:r + 1], bias=shift2[:, u, r:r + 1])
                last.then_inc(fin.out_made, 1)

            steps(act, finish)

        @block.vector
        def _(dve):
            dve.wait_ge(loaded, 16 * 14)
            dve.wait_ge(consts_made, 6)
            count = [0]

            def link(ins):
                count[0] += 1
                ins.then_inc(index_step, 1)
                dve.wait_ge(index_step, count[0])

            def to_put(n, take):
                link(nc.vector.tensor_tensor(put_f[:], put_f[:], spare_f[:], ALU.subtract))
                link(nc.vector.tensor_tensor(put_f[:], put_f[:], take, ALU.mult))
                link(nc.vector.tensor_tensor(put_f[:], put_f[:], spare_f[:], ALU.add))
                nc.vector.tensor_copy(put[n][:], put_f[:]).then_inc(puts_made, 1)

            nc.vector.tensor_copy(src_f[:], src_i[:, 0:TILES])
            nc.vector.tensor_copy(dst_f[:], dst_i[:, 0:TILES])
            nc.vector.tensor_copy(spare_f[:], spare_i[:])
            nc.vector.memset(msg_max[:, 1, GE - 1:GE], NEG)
            link(nc.vector.tensor_copy(next_f[:], next_i[:]))
            link(nc.vector.tensor_tensor(next_f[:], dst_f[:], next_f[:], ALU.not_equal))
            link(nc.vector.tensor_copy(put_f[:], dst_f[:]))
            to_put(0, next_f[:])
            link(nc.vector.tensor_scalar(put_f[:], put_f[:], 2.0, None, ALU.mult))
            nc.vector.tensor_copy(put[1][:], put_f[:]).then_inc(puts_made, 1)

            for L in layers:
                n = L.n

                def body(s, L=L, n=n):
                    u = s.u
                    if n == 1:
                        wait(dve, L.gathered[u], s.times(1, GATHERED))
                        nc.vector.scalar_tensor_tensor(gath[:, u, :, 0:D], gath[:, u, :, 0:D], SLOPE, gath[:, u, :, 0:D],
                                                       ALU.mult, ALU.max).then_inc(L.gath_ready, 1)
                        wait(dve, L.nodes_in[u], s.times(1, 2 * NODE_DMAS))
                        nc.vector.scalar_tensor_tensor(node_in[:, u], node_in[:, u], SLOPE, node_in[:, u],
                                                       ALU.mult, ALU.max).then_inc(L.node_ready, 1)
                    wait(dve, L.cut_scaled, s.at(1))
                    wait(dve, L.max_done, s.at(-1))
                    nc.vector.tensor_tensor(cut[:, u, :], dst_scaled[:, u, 0:GE], dst_scaled[:, u, 1:GE + 1],
                                            ALU.subtract).then_inc(L.cut_made, 1)
                    wait(dve, L.msg_done, s.at(1))
                    wait(dve, L.cut_made, s.at(1))
                    wait(dve, L.max_done, s.at(0))
                    wait(dve, L.back_done, s.at(-1))
                    nc.vector.tensor_tensor_scan(msg_max[:, u, :], cut[:, u, :], bank[2][0:D, 0:GE],
                                                 msg_max[:, 1 - u, GE - 1:GE], ALU.add, ALU.max).then_inc(L.max_done, 1)
                    for h in range(2):
                        wait(dve, L.root_done[h], s.at(1))
                        if h == 0:
                            if n == 0:
                                wait(dve, L.y_stored[u], s.times(0, NODE_DMAS))
                            to = y_out if n == 0 else zx_out
                        nc.vector.tensor_tensor(to[:, u, h * HALF:(h + 1) * HALF, 0:D],
                                                bank[6 + h][0:P, 0:HALF * D].rearrange("p (r d) -> p r d", d=D),
                                                bias_b[n][:, None, :].to_broadcast([P, HALF, D]),
                                                ALU.add).then_inc(L.y_made[h], 1)
                    if n == 0:
                        wait(dve, L.rows_in[u], s.times(1, 32))
                        for j in range(TG):
                            k = s.at(0) * TG + j
                            if j == 0:
                                wait(dve, L.sames_counted, s.at(0))
                            last = nc.vector.scalar_tensor_tensor(
                                same[:, j, :], src_row[:, u, :], src_f[:, bass.ds(k, 1)], earlier[:, j, :],
                                ALU.is_equal, ALU.mult, accum_out=earlier_count[:, bass.ds(k, 1)])
                        last.then_inc(L.sames_counted, 1)

                if n == 1:
                    dve.wait_ge(layers[0].back_done, GROUPS)
                    link(nc.vector.memset(msg_max[:, 1, GE - 1:GE], NEG))
                steps(dve, body)
                if n == 0:
                    dve.wait_ge(L.sames_counted, GROUPS)
                    link(nc.vector.tensor_scalar(earlier_count[:], earlier_count[:], 0.0, None, ALU.is_equal))
                    link(nc.vector.tensor_copy(put_f[:], src_f[:]))
                    to_put(2, earlier_count[:])

            for u in range(2):
                dve.wait_ge(layers[1].put_done[u], 16 * TG * GROUPS // 2)

            def variance(m, u, s, stat_steps, into, done):
                nc.vector.tensor_tensor(apart[:], m[:, :, 1], m[:, :, 4], ALU.subtract)
                nc.vector.tensor_tensor(squares[:], m[:, :, 2], m[:, :, 5], ALU.add)
                nc.vector.tensor_tensor(mean2[:, u, :], m[:, :, 1], m[:, :, 4], ALU.add).then_inc(stat_steps[0], 1)
                dve.wait_ge(stat_steps[0], s.at(1))
                nc.vector.scalar_tensor_tensor(apart[:], apart[:], 0.25, apart[:], ALU.mult, ALU.mult)
                nc.vector.tensor_scalar(squares[:], squares[:], 1.0 / D, EPS, ALU.mult, ALU.add).then_inc(stat_steps[1], 1)
                dve.wait_ge(stat_steps[1], s.at(1))
                nc.vector.tensor_tensor(into[:, u, :], apart[:], squares[:], ALU.add).then_inc(done, 1)

            def attend(s):
                u = s.u
                wait(dve, att.gathered[u], s.times(1, 16 * 2 * TG))
                wait(dve, att.x1_made, s.at(-1))
                nc.vector.scalar_tensor_tensor(pre[:, u], g_both[:, u, :, 0:D], SLOPE, g_both[:, u, :, 0:D],
                                               ALU.mult, ALU.max).then_inc(att.leaky_made, 1)
                dve.wait_ge(att.leaky_made, s.at(1))
                nc.vector.tensor_tensor(pre[:, u], pre[:, u], g_both[:, u, :, D:2 * D], ALU.add).then_inc(att.taken, 1)
                dve.wait_ge(att.taken, s.at(1))
                for j in range(2 * TG):
                    last = nc.vector.bn_stats(moments[:, u, j, :], pre[:, u, j, :])
                last.then_inc(att.moments_made, 1)
                dve.wait_ge(att.moments_made, s.at(1))
                variance(moments[:, u], u, s, att.stats_made, var_eps, att.var_made)
                wait(dve, att.rows_in[u], s.times(1, 16))
                wait(dve, att.sums_done, s.at(0))
                for j in range(TG):
                    k = s.at(0) * TG + j
                    last = nc.vector.tensor_scalar(same[:, j, :], src_row[:, u, :], src_f[:, bass.ds(k, 1)], None,
                                                   ALU.is_equal)
                last.then_inc(att.same_made, 1)
                wait(dve, att.rstd_made, s.at(1))
                nc.vector.scalar_tensor_tensor(shift[:, u, :], mean2[:, u, :], -0.5, rstd[:, u, :],
                                               ALU.mult, ALU.mult).then_inc(att.shift_made, 1)
                wait(dve, att.q_copied, s.at(1))
                for h in range(2):
                    last = nc.vector.tensor_tensor(
                        prod[:, 2 * h:2 * h + 2, :], q_sb[:, 2 * h:2 * h + 2, :],
                        bank[3 + h][0:P, 0:4 * D].rearrange("p (j d) -> p j d", d=2 * D)[:, :, 0:D], ALU.mult)
                last.then_inc(att.prod_made, 1)
                dve.wait_ge(att.prod_made, s.at(1))
                nc.vector.tensor_reduce(scores[:].rearrange("p j h -> p (j h)"),
                                        prod[:].rearrange("p j (h d) -> p (j h) d", d=DH), AX.X,
                                        ALU.add).then_inc(att.score_made, 1)
                dve.wait_ge(att.score_made, s.at(1))
                wait(dve, att.exp_made, s.at(0))
                nc.vector.tensor_scalar(clipped[:], scores[:], -10.0, 10.0, ALU.max, ALU.min).then_inc(att.clip_made, 1)
                wait(dve, att.exp_made, s.at(1))
                for j in range(TG):
                    last = nc.vector.tensor_tensor(
                        vals[:, u, j, 0:D].rearrange("p (h d) -> p h d", d=DH),
                        bank[3 + j // 2][0:P, (j % 2) * 2 * D + D:(j % 2 + 1) * 2 * D].rearrange("p (h d) -> p h d", d=DH),
                        vals[:, u, j, D:DV][:, :, None].to_broadcast([P, HEADS, DH]), ALU.mult)
                last.then_inc(att.val_made, 1)

            steps(dve, attend)
            for u in range(2):
                dve.wait_ge(att.put_done[u], 16 * TG * GROUPS // 2)

            def finish(s):
                u = s.u
                wait(dve, fin.blocks_in[u], s.times(1, 2 * NODE_DMAS))
                wait(dve, fin.x1_made, s.at(-1))
                nc.vector.scalar_tensor_tensor(pre[:, u], zx_out[:, u, :, 0:D], SLOPE, zx_out[:, u, :, 0:D],
                                               ALU.mult, ALU.max).then_inc(fin.leaky_made, 1)
                dve.wait_ge(fin.leaky_made, s.at(1))
                nc.vector.tensor_tensor(pre[:, u], pre[:, u], zx_out[:, u, :, D:2 * D], ALU.add).then_inc(fin.pre_made, 1)
                nc.vector.tensor_scalar(den[:], fin_sums[:, u, :, D:DV], 1e-8, None, ALU.add).then_inc(fin.norm_made, 1)
                dve.wait_ge(fin.norm_made, s.at(1))
                for r in range(ROWS):
                    last = nc.vector.bn_stats(moments[:, u, r, :], pre[:, u, r, :])
                last.then_inc(fin.moments_made, 1)
                nc.vector.reciprocal(inv_den[:], den[:]).then_inc(fin.inv_made, 1)
                dve.wait_ge(fin.inv_made, s.at(1))
                variance(moments[:, u], u, s, fin.stats_made, var_eps, fin.var_made)
                nc.vector.tensor_tensor(fin_sums[:, u, :, 0:D].rearrange("p r (h d) -> p r h d", d=DH),
                                        fin_sums[:, u, :, 0:D].rearrange("p r (h d) -> p r h d", d=DH),
                                        inv_den[:, :, :, None].to_broadcast([P, ROWS, HEADS, DH]), ALU.mult).then_inc(fin.res_made, 1)
                wait(dve, fin.rstd_made, s.at(1))
                nc.vector.scalar_tensor_tensor(shift[:, u, :], mean2[:, u, :], -0.5, rstd[:, u, :],
                                               ALU.mult, ALU.mult).then_inc(fin.shift_made, 1)
                wait(dve, fin.x1_made, s.at(1))
                nc.vector.scalar_tensor_tensor(x1[:, u], x1[:, u], 2.0, fin_sums[:, u, :, 0:D], ALU.mult, ALU.add).then_inc(fin.sum_made, 1)
                dve.wait_ge(fin.sum_made, s.at(1))
                for r in range(ROWS):
                    last = nc.vector.bn_stats(moments2[:, u, r, :], x1[:, u, r, :])
                last.then_inc(fin.moments2_made, 1)
                dve.wait_ge(fin.moments2_made, s.at(1))
                variance(moments2[:, u], u, s, fin.stats2_made, var_eps2, fin.var2_made)
                wait(dve, fin.rstd2_made, s.at(1))
                wait(dve, fin.out_made, s.at(-1))
                nc.vector.scalar_tensor_tensor(shift2[:, u, :], mean2[:, u, :], -0.5, rstd2[:, u, :],
                                               ALU.mult, ALU.mult).then_inc(fin.shift2_made, 1)

            steps(dve, finish)

        @block.tensor
        def _(pe):
            pe.wait_ge(loaded, 16 * 14)
            pe.wait_ge(consts_made, 6)
            for L in layers:
                n = L.n

                def body(s, L=L, n=n):
                    u = s.u

                    def transpose_nodes(h):
                        if h == 0:
                            if n == 0:
                                wait(pe, L.nodes_in[u], s.times(1, NODE_DMAS))
                            else:
                                wait(pe, L.node_ready, s.at(1))
                        wait(pe, L.nodeT_copied[h], s.at(0))
                        for r in range(HALF):
                            last = nc.tensor.transpose(bank[4 + h][0:D, r * P:(r + 1) * P],
                                                       node_in[:, u, h * HALF + r, :], ident[0:P, 0:P])
                        last.then_inc(L.node_taken[h], 1)

                    def root(h):
                        wait(pe, L.nodeT_copied[h], s.at(1))
                        wait(pe, L.y_made[h], s.at(0))
                        for r in range(HALF):
                            last = nc.tensor.matmul(bank[6 + h][0:P, r * D:(r + 1) * D], nodeT[:, h, r * P:(r + 1) * P],
                                                    wroot[n][:], start=True, stop=True)
                        last.then_inc(L.root_done[h], 1)

                    if n == 0:
                        wait(pe, L.gathered[u], s.times(1, GATHERED))
                    else:
                        wait(pe, L.gath_ready, s.at(1))
                    wait(pe, L.attr_in[u], s.times(1, 16))
                    wait(pe, L.featT_copied, s.at(-1))
                    for j in range(TG):
                        last = nc.tensor.transpose(bank[u][:, j * P:(j + 1) * P], gath[:, u, j, :], ident[0:P, 0:P])
                    last.then_inc(L.feat_taken, 1)
                    transpose_nodes(0)
                    wait(pe, L.featT_copied, s.at(1))
                    wait(pe, L.max_done, s.at(0))
                    nc.tensor.matmul(bank[2][0:D, 0:GE], wcat[n][:], featT[:, u, :], start=True,
                                     stop=True).then_inc(L.msg_done, 1)
                    transpose_nodes(1)
                    root(0)
                    root(1)
                    wait(pe, L.max_done, s.at(1))
                    wait(pe, L.rows_kept, s.at(0))
                    for j in range(TG):
                        last = nc.tensor.transpose(bank[3][0:P, j * D:(j + 1) * D], msg_max[:, u, j * P:(j + 1) * P],
                                                   ident[0:D, 0:D])
                    last.then_inc(L.back_done, 1)

                steps(pe, body)

            pe.wait_ge(layers[1].rows_kept, GROUPS)
            pe.wait_ge(layers[1].max_done, GROUPS)
            pe.wait_ge(layers[1].y_made[1], GROUPS)

            def attend(s):
                u = s.u
                wait(pe, att.x1_made, s.at(1))
                wait(pe, att.x1T_copied, s.at(0))
                for j in range(2 * TG):
                    last = nc.tensor.transpose(bank[j // TG][0:D, (j % TG) * P:(j % TG + 1) * P], x1[:, u, j, :],
                                               ident[0:P, 0:P])
                last.then_inc(att.x1T_done, 1)
                wait(pe, att.x1T_copied, s.at(1))
                wait(pe, att.q_copied, s.at(0))
                wait(pe, att.val_made, s.at(0))
                for j in range(TG):
                    nc.tensor.matmul(bank[2][0:P, j * D:(j + 1) * D], x1T[:, 0, j * P:(j + 1) * P], wq[:],
                                     start=True, stop=True)
                    last = nc.tensor.matmul(bank[3 + j // 2][0:P, (j % 2) * 2 * D:(j % 2 + 1) * 2 * D],
                                            x1T[:, 1, j * P:(j + 1) * P], wkv[:], start=True, stop=True)
                last.then_inc(att.qkv_done, 1)
                wait(pe, att.val_made, s.at(1))
                wait(pe, att.same_made, s.at(1))
                wait(pe, att.sums_staged, s.at(0))
                for b in range(TG):
                    for a in range(TG):
                        last = nc.tensor.matmul(bank[5][0:P, b * DV:(b + 1) * DV], same[:, a, b * P:(b + 1) * P],
                                                vals[:, u, a, :], start=(a == 0), stop=(a == TG - 1))
                last.then_inc(att.sums_done, 1)

            steps(pe, attend)


def kernel(x, src, dst, edge_attr_32, L0_gnn_W1_msg, L0_gnn_W1_edge, L0_gnn_W1_root, L0_gnn_b1,
           L0_gnn_W2_msg, L0_gnn_W2_edge, L0_gnn_W2_root, L0_gnn_b2, L1_gnn_qW, L1_gnn_kW, L1_gnn_vW):
    import numpy as np
    import concourse.bacc as bacc
    from concourse.bass_utils import run_bass_kernel_spmd

    tile = 125
    src, dst = np.asarray(src), np.asarray(dst)
    arrays = {
        "x": x, "edge_attr": edge_attr_32,
        "src_tiles": src.reshape(-1, tile).T, "dst_tiles": dst.reshape(-1, tile).T,
        "dst_next_tiles": np.concatenate([dst[1:], np.full(1, -1, dst.dtype)]).reshape(-1, tile).T,
        "src_line": src,
        "dst_line": np.concatenate([dst[:1], dst]),
        "w1_msg": L0_gnn_W1_msg, "w2_msg": L0_gnn_W2_msg, "w1_edge": L0_gnn_W1_edge, "w2_edge": L0_gnn_W2_edge,
        "w1_root": L0_gnn_W1_root, "w2_root": L0_gnn_W2_root, "b1": L0_gnn_b1, "b2": L0_gnn_b2,
        "w_q": L1_gnn_qW, "w_k": L1_gnn_kW, "w_v": L1_gnn_vW,
    }
    nc = bacc.Bacc("TRN2", target_bir_lowering=False, num_devices=1)
    arrays = {k: np.ascontiguousarray(v) for k, v in arrays.items()}
    ap = {k: nc.dram_tensor(k, v.shape, mybir.dt.from_np(v.dtype), kind="ExternalInput").ap() for k, v in arrays.items()}
    out = nc.dram_tensor("out", arrays["x"].shape, F32, kind="ExternalOutput").ap()
    gnn_program(nc, ap["x"], ap["edge_attr"], ap["src_tiles"], ap["dst_tiles"], ap["dst_next_tiles"],
                ap["src_line"], ap["dst_line"], (ap["w1_msg"], ap["w2_msg"]), (ap["w1_edge"], ap["w2_edge"]),
                (ap["w1_root"], ap["w2_root"]), (ap["b1"], ap["b2"]), ap["w_q"], ap["w_k"], ap["w_v"], out)
    r = run_bass_kernel_spmd(nc, [arrays], core_ids=[0])
    return r.results[0]["out"]
```

```python
import concourse.bass as bass
from concourse import mybir
from contextlib import ExitStack

F32 = mybir.dt.float32
I32 = mybir.dt.int32
ALU = mybir.AluOpType
ACT = mybir.ActivationFunctionType
AX = mybir.AxisListType


class Step:

    def __init__(self, eng, turn, k, kept, last):
        self.eng, self.turn, self.k, self.kept, self.last = eng, turn, k, kept, last
        self.u = k % 2

    def back(self, n):
        return Step(self.eng, self.turn, self.k - n, self.kept, self.last)

    def was_loaded_ahead(self):
        return isinstance(self.turn, int) and 2 * self.turn + self.k < 2

    def exists(self):
        return not isinstance(self.turn, int) or 0 <= 2 * self.turn + self.k < self.last

    def of_turn(self, mult, plus):
        if isinstance(self.turn, int):
            return self.turn * mult + plus
        if (mult, plus) not in self.kept:
            self.kept[mult, plus] = self.eng.snap(self.turn * mult + plus)
        return self.kept[mult, plus]

    def value(self, mult, plus):
        return self.of_turn(2 * mult, self.k * mult + plus)

    def at(self, plus):
        return self.value(1, plus)

    def uses(self, plus, each):
        return self.of_turn(each, (self.k // 2 + plus) * each)


def wait(eng, s, value):
    if isinstance(value, int) and value <= 0:
        return
    eng.wait_ge(s, value)


def pipeline(eng, groups, lag, body):
    first = (lag + 3) // 2
    for g in range(2 * first):
        body(Step(eng, g // 2, g % 2, {}, groups))
    with eng.Fori(first, groups // 2) as t:
        kept = {}
        for k in range(2):
            body(Step(eng, t, k, kept, groups))
    for g in range(groups, groups + lag):
        body(Step(eng, g // 2, g % 2, {}, groups))


def gnn_program(nc, x, x_columns, edge_attr, src_tiles, dst_tiles, dst_next_tiles, src_line, dst_line,
                w_msg, w_edge, w_root, bias, w_q, w_k, w_v, out):
    N, D = x.shape
    E, DE = edge_attr.shape
    P = 125
    TILES = E // P
    TG = 4
    GROUPS = TILES // TG
    GE = TG * P
    ROWS = N // (GROUPS * P)
    HALF = ROWS // 2
    BLOCK = P * ROWS
    LAST_ROWS = 20
    LAST_BLOCK = P * LAST_ROWS
    LAST_BLOCKS = N // LAST_BLOCK
    HEADS = 4
    DH = D // HEADS
    DV = D + HEADS
    SLOTS = 2 * TG
    SPARE = SLOTS * P
    SPLIT = 80
    SLOPE = 0.01
    EPS = 1e-5
    NORM_EPS = 1e-8
    CLIP = 10.0
    NEG = -3.0e38
    STEP = 3.0e33
    assert TILES * P == E and GROUPS * TG == TILES and BLOCK * GROUPS == N and GROUPS % 2 == 0
    assert LAST_BLOCKS * LAST_BLOCK == N and LAST_BLOCKS % 2 == 0
    assert HEADS * DH == D and D + DE == 128 and ROWS == 2 * TG and 2 * GE == BLOCK

    y1_table = nc.dram_tensor("y1_table", (N + SPARE, D), F32, kind="Internal").ap()
    z2x_table = nc.dram_tensor("z2x_table", (N + SPARE, 2 * D), F32, kind="Internal").ap()
    z2_rows = z2x_table.rearrange("n (two d) -> (n two) d", two=2)
    x1_table = nc.dram_tensor("x1_table", (N, D), F32, kind="Internal").ap()
    sum_table = nc.dram_tensor("sum_table", (N + SPARE, DV), F32, kind="Internal").ap()

    ctx = ExitStack()
    with ctx:
        def sb(name, shape, dt=F32):
            return ctx.enter_context(nc.sbuf_tensor(name, shape, dt))

        def sem(name):
            return ctx.enter_context(nc.semaphore(name))

        def pair(name):
            return [sem(f"{name}_{u}") for u in range(2)]

        bank = [ctx.enter_context(nc.psum_tensor(f"bank{i}", [128, 512], F32)) for i in range(8)]

        ident = sb("ident", [128, 128])
        eps = sb("eps", [128, 1])
        wcat = [sb(f"wcat{i}", [128, D]) for i in range(2)]
        wroot = [sb(f"wroot{i}", [D, D]) for i in range(2)]
        bias_b = [sb(f"bias_b{i}", [P, D]) for i in range(2)]
        wqkv = sb("wqkv", [D, 3 * D])
        mean_of = sb("mean_of", [D, D])
        src_i = sb("src_i", [P, TILES + SLOTS], I32)
        dst_i = sb("dst_i", [P, TILES + SLOTS], I32)
        next_i = sb("next_i", [P, TILES], I32)
        src_f = sb("src_f", [P, TILES])
        dst_f = sb("dst_f", [P, TILES])
        next_f = sb("next_f", [P, TILES])
        spare_i = sb("spare_i", [P, TILES], I32)
        spare_f = sb("spare_f", [P, TILES])
        put = [sb(f"put{i}", [P, TILES], I32) for i in range(3)]
        put_f = sb("put_f", [P, TILES])
        earlier_count = sb("earlier_count", [P, TILES])
        earlier = sb("earlier", [P, TG, GE])
        zeros = sb("zeros", [P, ROWS, DV])
        take_src = sb("take_src", [P, SLOTS], I32)
        take_dst = sb("take_dst", [P, SLOTS], I32)
        put_idx = sb("put_idx", [P, SLOTS], I32)
        gath = sb("gath", [P, 2, TG, D + DE])
        put_rows = sb("put_rows", [P, 2, TG, D])
        featT = sb("featT", [128, 2, GE])
        msg_max = sb("msg_max", [D, 2, GE])
        dst_row = sb("dst_row", [D, 2, GE + 1], I32)
        dst_scaled = sb("dst_scaled", [D, 2, GE + 1])
        cut = sb("cut", [D, 2, GE])
        src_row = sb("src_row", [128, 2, GE], I32)
        same = sb("same", [P, TG, GE])
        node_in = sb("node_in", [P, 2, ROWS, D])
        nodeT = sb("nodeT", [D, 2, HALF * P])
        y_out = sb("y_out", [P, 2, ROWS, D])
        x_cols = same[0:D, :, :].rearrange("d (u h) e -> d u (h e)", u=2)
        kept_rows = sb("kept_rows", [P, TILES, D + DE])

        room = kept_rows[:, :, :].rearrange("p t d -> p (t d)")

        def carver():
            at = [0]

            def carve(*shape):
                size = 1
                for n in shape:
                    size *= n
                v = room[:, at[0]:at[0] + size]
                at[0] += size
                assert at[0] <= TILES * (D + DE)
                if len(shape) == 1:
                    return v
                if len(shape) == 2:
                    return v.rearrange("p (a b) -> p a b", b=shape[1])
                return v.rearrange("p (a b c) -> p a b c", b=shape[1], c=shape[2])

            return carve

        carve = carver()
        ends = carve(2, 2 * TG, 2 * D)
        ends_pre = carve(2, 2 * TG, D)
        endsT = carve(2, GE)
        nodes_zx = carve(2, ROWS, 2 * D)
        nodes_pre = carve(2, ROWS, D)
        moments = carve(2, 2 * TG + ROWS, 6)
        apart = carve(2 * TG + ROWS)
        squares = carve(2 * TG + ROWS)
        mean2 = carve(2, 2 * TG + ROWS)
        var = carve(2, 2 * TG + ROWS)
        std = carve(2, 2 * TG + ROWS)
        rstd = carve(2, 2 * TG + ROWS)
        shift = carve(2, ROWS)
        both_rstd = carve(2, TG)
        q_sb = carve(2, TG, D)
        prod = carve(TG, D)
        scores = carve(TG, HEADS)
        clipped = carve(TG, HEADS)
        weight_rstd = carve(TG, HEADS)
        vals = carve(2, TG, DV)
        sums = carve(2, TG, DV)
        carve = carver()
        last_x1 = carve(2, LAST_ROWS, D)
        last_sums = carve(2, LAST_ROWS, DV)
        last_pre = carve(2, LAST_ROWS, D)
        last_out = carve(2, LAST_ROWS, D)
        den = carve(LAST_ROWS, HEADS)
        inv_den = carve(2, LAST_ROWS * HEADS)
        last_moments = carve(2, LAST_ROWS, 6)
        last_apart = carve(LAST_ROWS)
        last_squares = carve(LAST_ROWS)
        last_mean2 = carve(2, LAST_ROWS)
        last_var = carve(2, LAST_ROWS)
        last_std = carve(2, LAST_ROWS)
        last_rstd = carve(2, LAST_ROWS)
        last_shift = carve(2, LAST_ROWS)

        src_loaded = sem("src_loaded")
        loaded = sem("loaded")
        zero_set = sem("zero_set")
        spares_zeroed = sem("spares_zeroed")
        sums_zeroed = sem("sums_zeroed")
        x_copied = sem("x_copied")
        attr_in = sem("attr_in")
        consts_made = sem("consts_made")
        index_steps = sem("index_steps")
        puts_made = sem("puts_made")
        means_made = sem("means_made")
        centered = sem("centered")
        sp_turns = sem("sp_turns")
        pool_turns = sem("pool_turns")

        class Layer:
            def __init__(self, n):
                self.n = n
                self.idx_staged = sem(f"layer{n}_idx_staged")
                self.nodes_leaky = sem(f"layer{n}_nodes_leaky")
                self.rows_kept = sem(f"layer{n}_rows_kept")
                self.restaged = sem(f"layer{n}_restaged")
                self.feat_done = sem(f"layer{n}_feat_done")
                self.featT_made = sem(f"layer{n}_featT_made")
                self.dst_scaled = sem(f"layer{n}_dst_scaled")
                self.cut_made = sem(f"layer{n}_cut_made")
                self.msg_done = sem(f"layer{n}_msg_done")
                self.max_done = sem(f"layer{n}_max_done")
                self.back_done = sem(f"layer{n}_back_done")
                self.put_staged = sem(f"layer{n}_put_staged")
                self.nodeT_done = pair(f"layer{n}_nodeT_done")
                self.nodeT_made = pair(f"layer{n}_nodeT_made")
                self.root_done = pair(f"layer{n}_root_done")
                self.y_made = pair(f"layer{n}_y_made")
                self.gathered = pair(f"layer{n}_gathered")
                self.dst_in = pair(f"layer{n}_dst_in")
                self.nodes_in = pair(f"layer{n}_nodes_in")
                self.y_stored = pair(f"layer{n}_y_stored")
                self.put_done = pair(f"layer{n}_put_done")

        class Attention:
            def __init__(self):
                self.idx_staged = sem("att_idx_staged")
                self.ends_leaky = sem("att_ends_leaky")
                self.ends_made = sem("att_ends_made")
                self.ends_measured = sem("att_ends_measured")
                self.nodes_leaky = sem("att_nodes_leaky")
                self.nodes_made = sem("att_nodes_made")
                self.nodes_measured = sem("att_nodes_measured")
                self.halves_added = sem("att_halves_added")
                self.spread_made = sem("att_spread_made")
                self.var_made = sem("att_var_made")
                self.std_made = sem("att_std_made")
                self.rstd_made = sem("att_rstd_made")
                self.ends_scaled = sem("att_ends_scaled")
                self.shift_made = sem("att_shift_made")
                self.endsT_done = sem("att_endsT_done")
                self.endsT_made = sem("att_endsT_made")
                self.qkv_done = sem("att_qkv_done")
                self.q_copied = sem("att_q_copied")
                self.prod_made = sem("att_prod_made")
                self.score_made = sem("att_score_made")
                self.scaled_made = sem("att_scaled_made")
                self.clip_made = sem("att_clip_made")
                self.exp_made = sem("att_exp_made")
                self.weight_made = sem("att_weight_made")
                self.val_made = sem("att_val_made")
                self.same_made = sem("att_same_made")
                self.sums_done = sem("att_sums_done")
                self.sums_staged = sem("att_sums_staged")
                self.x1_made = sem("att_x1_made")
                self.gathered = pair("att_gathered")
                self.src_in = pair("att_src_in")
                self.nodes_in = pair("att_nodes_in")
                self.x1_stored = pair("att_x1_stored")
                self.put_done = pair("att_put_done")

        class LastLoop:
            def __init__(self):
                self.den_made = sem("last_den_made")
                self.inv_made = sem("last_inv_made")
                self.res_made = sem("last_res_made")
                self.pre_made = sem("last_pre_made")
                self.measured = sem("last_measured")
                self.halves_added = sem("last_halves_added")
                self.spread_made = sem("last_spread_made")
                self.var_made = sem("last_var_made")
                self.std_made = sem("last_std_made")
                self.rstd_made = sem("last_rstd_made")
                self.shift_made = sem("last_shift_made")
                self.out_made = sem("last_out_made")
                self.blocks_in = pair("last_blocks_in")
                self.stored = pair("last_stored")

        layers = [Layer(0), Layer(1)]
        att = Attention()
        last = LastLoop()
        sames_counted = sem("sames_counted")
        sames_in = pair("sames_in")

        NODE_DMAS = 32
        GATHERED = 16 * TG
        BOTH_GATHERED = 2 * GATHERED
        ALL_PUT = GATHERED * GROUPS // 2
        ALL_NODES = NODE_DMAS * GROUPS // 2
        LOADS = 14
        OTHER_LOADS = LOADS - 1

        def node_parts(table, row, rows=ROWS, columns=slice(None)):
            v = table[bass.ds(row, P * rows), columns].rearrange("(p r) d -> p r d", r=rows)
            return [(v[a:b], a, b) for a, b in ((0, SPLIT), (SPLIT, P))]

        block = ctx.enter_context(nc.Block())

        @block.sync
        def _(sp):
            loads = [(wqkv[:, 0:D], w_q), (wqkv[:, D:2 * D], w_k), (wqkv[:, 2 * D:3 * D], w_v),
                     (src_i[:, 0:TILES], src_tiles), (dst_i[:, 0:TILES], dst_tiles), (next_i[:, :], dst_next_tiles)]
            for n in range(2):
                loads += [(wcat[n][0:D, :], w_msg[n]), (wcat[n][D:D + DE, :], w_edge[n]), (wroot[n][:, :], w_root[n]),
                          (bias_b[n][:, :], bias[n][None, :].to_broadcast([P, D]))]
            assert len(loads) == LOADS
            to, of = loads[3]
            sp.dma_start(to, of).then_inc(src_loaded, 16)
            for to, of in loads[4:6] + loads[0:3] + loads[6:]:
                sp.dma_start(to, of).then_inc(loaded, 16)

            sp.wait_ge(zero_set, 1)
            for table, width in ((y1_table, D), (z2x_table[:, 0:D], D), (sum_table, DV)):
                sp.dma_start(table[N:N + SPARE, :].rearrange("(p r) d -> p r d", r=SLOTS),
                             zeros[:, :, 0:width]).then_inc(spares_zeroed, 16)

            def load_lines(s, L, n):
                edge = s.value(GE, 0)
                wait(sp, L.dst_scaled, s.at(-1))
                sp.sem_inc(sp_turns, 1)
                sp.dma_start(dst_row[:, s.u, :], dst_line[bass.ds(edge, GE + 1)][None, :].to_broadcast([D, GE + 1])
                             ).then_inc(L.dst_in[s.u], 16)
                if n == 0:
                    wait(sp, sames_counted, s.at(-1))
                    sp.sem_inc(sp_turns, 1)
                    sp.dma_start(src_row[:, s.u, :], src_line[bass.ds(edge, GE)][None, :].to_broadcast([128, GE])
                                 ).then_inc(sames_in[s.u], 16)

            for L in layers:
                n = L.n

                def take(s, L=L, n=n):
                    if s.exists():
                        node, u = s.value(BLOCK, 0), s.u
                        if n == 0:
                            wait(sp, L.root_done[1], s.at(-1))
                            sp.sem_inc(sp_turns, 1)
                            sp.dma_start(x_cols[:, u, :], x_columns[:, bass.ds(node, BLOCK)]).then_inc(L.nodes_in[u], 16)
                            sp.dma_start(kept_rows[:, bass.ds(s.value(TG, 0), TG), D:D + DE],
                                         edge_attr[bass.ds(s.value(GE, 0), GE), :].rearrange("(j p) d -> p j d", p=P)
                                         ).then_inc(attr_in, 16)
                        else:
                            wait(sp, L.nodeT_done[1], s.at(-1))
                            for v, lo, hi in node_parts(y1_table, node):
                                sp.dma_start(node_in[lo:hi, u], v).then_inc(L.nodes_in[u], 16)
                    b = s.back(2)
                    if b.exists():
                        node = b.value(BLOCK, 0)
                        wait(sp, L.y_made[1], b.at(1))
                        for v, lo, hi in node_parts(y1_table if n == 0 else z2x_table, node, columns=slice(0, D)):
                            sp.dma_start(v, y_out[lo:hi, b.u]).then_inc(L.y_stored[b.u], 16)

                if n == 1:
                    for u in range(2):
                        sp.wait_ge(layers[0].put_done[u], ALL_PUT)
                    sp.wait_ge(layers[0].dst_scaled, GROUPS)
                for u in range(2):
                    load_lines(Step(sp, 0, u, {}, GROUPS), L, n)
                pipeline(sp, GROUPS, 2, take)

                def put_loads(s, L=L, n=n):
                    if not s.was_loaded_ahead():
                        load_lines(s, L, n)
                    node = s.value(BLOCK, 0)
                    half = s.value(BLOCK, n * BLOCK // 2)
                    sp.dma_start(z2x_table[bass.ds(half, BLOCK // 2), D:2 * D],
                                 x[bass.ds(half, BLOCK // 2), :]).then_inc(x_copied, 16)
                    if n == 1:
                        for v, lo, hi in node_parts(sum_table, node):
                            sp.dma_start(v, zeros[lo:hi]).then_inc(sums_zeroed, 16)

                pipeline(sp, GROUPS, 0, put_loads)

            for u in range(2):
                sp.wait_ge(layers[1].put_done[u], ALL_PUT)
            sp.wait_ge(x_copied, 2 * 16 * GROUPS)
            sp.wait_ge(sames_counted, GROUPS)

            def attend(s):
                if s.exists():
                    node, edge = s.value(BLOCK, 0), s.value(GE, 0)
                    wait(sp, att.nodes_made, s.at(-1))
                    for v, lo, hi in node_parts(z2x_table, node):
                        sp.dma_start(nodes_zx[lo:hi, s.u], v).then_inc(att.nodes_in[s.u], 16)
                    wait(sp, att.same_made, s.at(-1))
                    sp.sem_inc(sp_turns, 1)
                    sp.dma_start(src_row[:, s.u, :], src_line[bass.ds(edge, GE)][None, :].to_broadcast([128, GE])
                                 ).then_inc(att.src_in[s.u], 16)
                b = s.back(3)
                if b.exists():
                    node = b.value(BLOCK, 0)
                    wait(sp, att.x1_made, b.at(1))
                    for v, lo, hi in node_parts(x1_table, node):
                        sp.dma_start(v, y_out[lo:hi, b.u]).then_inc(att.x1_stored[b.u], 16)

            pipeline(sp, GROUPS, 3, attend)

            for u in range(2):
                sp.wait_ge(att.put_done[u], ALL_PUT)
                sp.wait_ge(att.x1_stored[u], ALL_NODES)

            def finish(s):
                if s.exists():
                    node = s.value(LAST_BLOCK, 0)
                    wait(sp, last.pre_made, s.at(-1))
                    for v, lo, hi in node_parts(sum_table, node, LAST_ROWS):
                        sp.dma_start(last_sums[lo:hi, s.u], v).then_inc(last.blocks_in[s.u], 16)
                    for v, lo, hi in node_parts(x1_table, node, LAST_ROWS):
                        sp.dma_start(last_x1[lo:hi, s.u], v).then_inc(last.blocks_in[s.u], 16)
                b = s.back(3)
                if b.exists():
                    node = b.value(LAST_BLOCK, 0)
                    wait(sp, last.out_made, b.at(1))
                    for v, lo, hi in node_parts(out, node, LAST_ROWS):
                        sp.dma_start(v, last_out[lo:hi, b.u]).then_inc(last.stored[b.u], 16)

            pipeline(sp, LAST_BLOCKS, 3, finish)
            for u in range(2):
                sp.wait_ge(last.stored[u], NODE_DMAS * LAST_BLOCKS // 2)

        @block.gpsimd
        def _(pool):
            nc.gpsimd.memset(zeros[:], 0.0).then_inc(zero_set, 1)
            nc.gpsimd.memset(ident[:], 0.0).then_inc(consts_made, 1)
            nc.gpsimd.memset(earlier[:], 1.0).then_inc(consts_made, 1)
            nc.gpsimd.memset(src_i[:, TILES:], 0)
            nc.gpsimd.memset(dst_i[:, TILES:], 0)
            nc.gpsimd.iota(spare_i[:, :].rearrange("p (a b) -> p a b", b=SLOTS),
                           pattern=[[0, TILES // SLOTS], [P, SLOTS]], base=N,
                           channel_multiplier=1).then_inc(consts_made, 1)
            nc.gpsimd.memset(eps[:], EPS)
            nc.gpsimd.memset(mean_of[:], 1.0 / D).then_inc(consts_made, 1)
            pool.wait_ge(consts_made, 4)
            nc.gpsimd.affine_select(out=ident[:], in_=ident[:], compare_op=ALU.not_equal, fill=1.0, base=0,
                                    pattern=[[-1, 128]], channel_multiplier=1).then_inc(consts_made, 1)
            nc.gpsimd.affine_select(out=earlier[:], in_=earlier[:], compare_op=ALU.is_gt, fill=0.0, base=0,
                                    pattern=[[P, TG], [-1, GE]], channel_multiplier=1).then_inc(consts_made, 1)

            def scatter(s, table, rows, done):
                for j in range(TG):
                    at = s.u * TG + j
                    pool.indirect_dma_start(
                        out=table, in_=rows[:, s.u, j, :], in_offset=None,
                        out_offset=bass.IndirectOffsetOnAxis(ap=put_idx[:, at:at + 1], axis=0),
                        compute_op=ALU.add).then_inc(done[s.u], 16)

            for L in layers:
                if L.n == 1:
                    for u in range(2):
                        pool.wait_ge(layers[0].put_done[u], ALL_PUT)

                def take(s, L=L, table=(x, y1_table)[L.n]):
                    wait(pool, L.rows_kept, s.at(-1))
                    wait(pool, L.idx_staged, s.at(1))
                    pool.sem_inc(pool_turns, 1)
                    for j in range(TG):
                        at = s.u * TG + j
                        pool.indirect_dma_start(
                            out=gath[:, s.u, j, 0:D], out_offset=None, in_=table[0:N, :],
                            in_offset=bass.IndirectOffsetOnAxis(ap=take_src[:, at:at + 1], axis=0),
                        ).then_inc(L.gathered[s.u], 16)

                pipeline(pool, GROUPS, 0, take)
                for u in range(2):
                    pool.wait_ge(L.y_stored[u], ALL_NODES)
                pool.wait_ge(spares_zeroed, 16 * 3)

                def put_rows_in(s, L=L, table=(y1_table, z2_rows)[L.n]):
                    wait(pool, L.put_staged, s.at(1))
                    pool.sem_inc(pool_turns, 1)
                    scatter(s, table, put_rows, L.put_done)

                pipeline(pool, GROUPS, 0, put_rows_in)

            for u in range(2):
                pool.wait_ge(layers[1].put_done[u], ALL_PUT)
            pool.wait_ge(x_copied, 2 * 16 * GROUPS)
            pool.wait_ge(sums_zeroed, NODE_DMAS * GROUPS)

            def attend(s):
                if s.exists():
                    wait(pool, att.ends_made, s.at(-1))
                    wait(pool, att.idx_staged, s.at(1))
                    pool.sem_inc(pool_turns, 1)
                    for j in range(2 * TG):
                        idx = take_src if j < TG else take_dst
                        at = s.u * TG + j % TG
                        pool.indirect_dma_start(
                            out=ends[:, s.u, j, :], out_offset=None, in_=z2x_table[0:N, :],
                            in_offset=bass.IndirectOffsetOnAxis(ap=idx[:, at:at + 1], axis=0),
                        ).then_inc(att.gathered[s.u], 16)
                b = s.back(3)
                if b.exists():
                    before = b.back(1)
                    if before.exists():
                        wait(pool, att.put_done[before.u], before.uses(1, GATHERED))
                    wait(pool, att.sums_staged, b.at(1))
                    pool.sem_inc(pool_turns, 1)
                    scatter(b, sum_table, sums, att.put_done)

            pipeline(pool, GROUPS, 3, attend)

            pool.wait_ge(att.x1_made, GROUPS)

            def finish(s):
                wait(pool, last.inv_made, s.at(1))
                sums_by_head = last_sums[:, s.u, :, 0:D].rearrange("p r (h d) -> p r h d", d=DH)
                nc.gpsimd.tensor_tensor(sums_by_head, sums_by_head,
                                        inv_den[:, s.u].rearrange("p (r h) -> p r h", h=HEADS)[:, :, :, None].to_broadcast([P, LAST_ROWS, HEADS, DH]),
                                        ALU.mult).then_inc(last.res_made, 1)

            pipeline(pool, LAST_BLOCKS, 0, finish)

        @block.scalar
        def _(act):
            act.wait_ge(src_loaded, 16)

            def copy_indices(s, plus, into, of):
                return nc.scalar.copy(into[:, s.u * TG:(s.u + 1) * TG], of[:, bass.ds(s.value(TG, plus * TG), TG)])

            def first_indices(pairs, done):
                for u in range(2):
                    for into, of in pairs:
                        copied = nc.scalar.copy(into[:, u * TG:(u + 1) * TG], of[:, u * TG:(u + 1) * TG])
                    copied.then_inc(done, 1)

            for L in layers:
                n = L.n

                if n == 1:
                    act.wait_ge(layers[0].rows_kept, GROUPS)
                first_indices([(take_src, src_i)], L.idx_staged)
                if n == 0:
                    act.wait_ge(loaded, 16 * OTHER_LOADS)
                    act.wait_ge(consts_made, 6)

                def take(s, L=L, n=n):
                    wait(act, L.gathered[s.u], s.uses(1, GATHERED))
                    copy_indices(s, 2, take_src, src_i).then_inc(L.idx_staged, 1)
                    if n == 1:
                        for h in range(2):
                            wait(act, L.nodeT_done[h], s.at(1))
                            wait(act, L.root_done[h], s.at(0))
                            nc.scalar.copy(nodeT[:, h, :], bank[4 + h][0:D, 0:HALF * P]).then_inc(L.nodeT_made[h], 1)

                pipeline(act, GROUPS, 0, take)
                act.wait_ge(puts_made, n + 1)

                def put_steps(s, L=L, n=n):
                    b = s.back(2)
                    if b.exists():
                        wait(act, L.back_done, b.at(1))
                        wait(act, L.put_done[b.u], b.uses(0, GATHERED))
                        copy_indices(b, 0, put_idx, put[n])
                        nc.scalar.copy(put_rows[:, b.u].rearrange("p j d -> p (j d)"),
                                       bank[3][0:P, 0:TG * D]).then_inc(L.put_staged, 1)
                    if s.exists():
                        wait(act, L.dst_in[s.u], s.uses(1, 16))
                        wait(act, L.cut_made, s.at(-1))
                        nc.scalar.activation(dst_scaled[:, s.u, :], dst_row[:, s.u, :], ACT.Copy,
                                             scale=STEP).then_inc(L.dst_scaled, 1)
                        wait(act, L.feat_done, s.at(1))
                        wait(act, L.msg_done, s.at(-1))
                        nc.scalar.copy(featT[:, s.u, :], bank[s.u][:, 0:GE]).then_inc(L.featT_made, 1)

                pipeline(act, GROUPS, 2, put_steps)

            act.wait_ge(puts_made, 3)
            for u in range(2):
                act.wait_ge(layers[1].put_done[u], ALL_PUT)
            first_indices([(take_src, src_i), (take_dst, dst_i)], att.idx_staged)

            def attend(s):
                b1, b2 = s.back(1), s.back(2)
                if s.exists():
                    wait(act, att.ends_leaky, s.at(1))
                    copy_indices(s, 2, take_src, src_i)
                    copy_indices(s, 2, take_dst, dst_i).then_inc(att.idx_staged, 1)
                if b2.exists():
                    wait(act, att.sums_done, b2.at(1))
                    wait(act, att.put_done[b2.u], b2.uses(0, GATHERED))
                    copy_indices(b2, 0, put_idx, put[2])
                    nc.scalar.copy(sums[:, b2.u].rearrange("p j d -> p (j d)"),
                                   bank[7][0:P, 0:TG * DV]).then_inc(att.sums_staged, 1)
                if s.exists():
                    wait(act, att.endsT_done, s.at(1))
                    wait(act, att.qkv_done, s.at(0))
                    for e in range(2):
                        copied = nc.scalar.copy(endsT[0:D, e, :], bank[e][0:D, 0:GE])
                    copied.then_inc(att.endsT_made, 1)
                if b1.exists():
                    wait(act, att.clip_made, b1.at(1))
                    wait(act, att.sums_done, b1.at(-1))
                    nc.scalar.activation(vals[:, b1.u, :, D:DV], clipped[:], ACT.Exp).then_inc(att.exp_made, 1)
                if s.exists():
                    wait(act, att.qkv_done, s.at(1))
                    wait(act, att.prod_made, s.at(-1))
                    nc.scalar.copy(q_sb[:, s.u].rearrange("p j d -> p (j d)"),
                                   bank[2][0:P, 0:TG * D]).then_inc(att.q_copied, 1)
                if s.exists():
                    wait(act, att.var_made, s.at(1))
                    nc.scalar.activation(std[:, s.u, :], var[:, s.u, :], ACT.Sqrt,
                                         bias=eps[0:P, 0:1]).then_inc(att.std_made, 1)
                if b1.exists():
                    wait(act, att.shift_made, b1.at(1))
                    wait(act, att.x1_stored[b1.u], b1.uses(0, NODE_DMAS))
                    for r in range(ROWS):
                        e = 2 * TG + r
                        made = nc.scalar.activation(y_out[:, b1.u, r, :], nodes_pre[:, b1.u, r, :], ACT.Identity,
                                                    scale=rstd[:, b1.u, e:e + 1], bias=shift[:, b1.u, r:r + 1])
                    made.then_inc(att.x1_made, 1)

            pipeline(act, GROUPS, 2, attend)

            def finish(s):
                u = s.u
                wait(act, last.var_made, s.at(1))
                nc.scalar.activation(last_std[:, u, :], last_var[:, u, :], ACT.Sqrt,
                                     bias=eps[0:P, 0:1]).then_inc(last.std_made, 1)
                wait(act, last.shift_made, s.at(1))
                wait(act, last.stored[u], s.uses(0, NODE_DMAS))
                for r in range(LAST_ROWS):
                    made = nc.scalar.activation(last_out[:, u, r, :], last_pre[:, u, r, :], ACT.Identity,
                                                scale=last_rstd[:, u, r:r + 1], bias=last_shift[:, u, r:r + 1])
                made.then_inc(last.out_made, 1)

            pipeline(act, LAST_BLOCKS, 0, finish)

        @block.vector
        def _(dve):
            dve.wait_ge(src_loaded, 16)
            dve.wait_ge(loaded, 16 * OTHER_LOADS)
            dve.wait_ge(consts_made, 6)
            count = [0]

            def link(ins):
                count[0] += 1
                ins.then_inc(index_steps, 1)
                dve.wait_ge(index_steps, count[0])

            def to_put(n, counts):
                link(nc.vector.tensor_tensor(put_f[:], put_f[:], spare_f[:], ALU.subtract))
                link(nc.vector.tensor_tensor(put_f[:], put_f[:], counts, ALU.mult))
                link(nc.vector.tensor_tensor(put_f[:], put_f[:], spare_f[:], ALU.add))
                nc.vector.tensor_copy(put[n][:], put_f[:]).then_inc(puts_made, 1)

            def index_work():
                nc.vector.tensor_copy(src_f[:], src_i[:, 0:TILES])
                nc.vector.tensor_copy(dst_f[:], dst_i[:, 0:TILES])
                nc.vector.tensor_copy(spare_f[:], spare_i[:])
                link(nc.vector.tensor_copy(next_f[:], next_i[:]))
                link(nc.vector.tensor_tensor(next_f[:], dst_f[:], next_f[:], ALU.not_equal))
                link(nc.vector.tensor_copy(put_f[:], dst_f[:]))
                to_put(0, next_f[:])
                link(nc.vector.tensor_scalar(put_f[:], put_f[:], 2.0, None, ALU.mult))
                nc.vector.tensor_copy(put[1][:], put_f[:]).then_inc(puts_made, 1)
                dve.wait_ge(means_made, 1)
                nc.vector.tensor_tensor(wqkv[:], wqkv[:], bank[0][0:D, 0:3 * D], ALU.subtract).then_inc(centered, 1)

            index_work()
            for L in layers:
                n = L.n

                def take(s, L=L, n=n):
                    if s.exists():
                        if n == 1:
                            wait(dve, L.nodes_in[s.u], s.uses(1, NODE_DMAS))
                            nc.vector.scalar_tensor_tensor(node_in[:, s.u], node_in[:, s.u], SLOPE, node_in[:, s.u],
                                                           ALU.mult, ALU.max).then_inc(L.nodes_leaky, 1)
                        wait(dve, L.gathered[s.u], s.uses(1, GATHERED))
                        kept = kept_rows[:, bass.ds(s.value(TG, 0), TG), 0:D]
                        if n == 0:
                            nc.vector.tensor_copy(kept, gath[:, s.u, :, 0:D]).then_inc(L.rows_kept, 1)
                        else:
                            nc.vector.scalar_tensor_tensor(kept, gath[:, s.u, :, 0:D], SLOPE, gath[:, s.u, :, 0:D],
                                                           ALU.mult, ALU.max).then_inc(L.rows_kept, 1)
                    b = s.back(n)
                    if b.exists():
                        for h in range(2):
                            wait(dve, L.root_done[h], b.at(1))
                            if h == 0:
                                wait(dve, L.y_stored[b.u], b.uses(0, NODE_DMAS))
                            nc.vector.tensor_tensor(y_out[:, b.u, h * HALF:(h + 1) * HALF, :],
                                                    bank[6 + h][0:P, 0:HALF * D].rearrange("p (r d) -> p r d", d=D),
                                                    bias_b[n][:, None, :].to_broadcast([P, HALF, D]),
                                                    ALU.add).then_inc(L.y_made[h], 1)

                if n == 1:
                    dve.wait_ge(layers[0].feat_done, GROUPS)
                pipeline(dve, GROUPS, n, take)
                if n == 0:
                    dve.wait_ge(attr_in, 16 * GROUPS)

                def put_steps(s, L=L, n=n):
                    if s.exists():
                        wait(dve, L.feat_done, s.at(-1))
                        wait(dve, L.rows_kept, s.at(1))
                        nc.vector.tensor_copy(gath[:, s.u], kept_rows[:, bass.ds(s.value(TG, 0), TG), :]).then_inc(L.restaged, 1)
                        if n == 0:
                            wait(dve, sames_in[s.u], s.uses(1, 16))
                            wait(dve, sames_counted, s.at(0))
                            for j in range(TG):
                                k = s.value(TG, j)
                                upto = (j + 1) * P
                                counted = nc.vector.scalar_tensor_tensor(
                                    same[:, j, 0:upto], src_row[0:P, s.u, 0:upto], src_f[:, bass.ds(k, 1)], earlier[:, j, 0:upto],
                                    ALU.is_equal, ALU.mult, accum_out=earlier_count[:, bass.ds(k, 1)])
                            counted.then_inc(sames_counted, 1)
                    b = s.back(1)
                    if b.exists():
                        wait(dve, L.dst_scaled, b.at(1))
                        wait(dve, L.max_done, b.at(-1))
                        nc.vector.tensor_tensor(cut[:, b.u, :], dst_scaled[:, b.u, 0:GE], dst_scaled[:, b.u, 1:GE + 1],
                                                ALU.subtract).then_inc(L.cut_made, 1)
                        wait(dve, L.msg_done, b.at(1))
                        wait(dve, L.back_done, b.at(-1))
                        wait(dve, L.cut_made, b.at(1))
                        wait(dve, L.max_done, b.at(0))
                        nc.vector.tensor_tensor_scan(msg_max[:, b.u, :], cut[:, b.u, :], bank[2][0:D, 0:GE],
                                                     msg_max[:, 1 - b.u, GE - 1:GE], ALU.add, ALU.max).then_inc(L.max_done, 1)

                if n == 1:
                    dve.wait_ge(layers[0].back_done, GROUPS)
                link(nc.vector.memset(msg_max[:, 1, GE - 1:GE], NEG))
                pipeline(dve, GROUPS, 1, put_steps)

            dve.wait_ge(sames_counted, GROUPS)
            link(nc.vector.tensor_scalar(earlier_count[:], earlier_count[:], 0.0, None, ALU.is_equal))
            link(nc.vector.tensor_copy(put_f[:], src_f[:]))
            to_put(2, earlier_count[:])

            def measure(rows, into, at, n, done):
                for r in range(n):
                    measured = nc.vector.bn_stats(into[:, at + r, :], rows[:, r, :])
                measured.then_inc(done, 1)

            def variance(s, sems, m, near, square, twice_mean, into):
                dve.wait_ge(sems[0], s.at(1))
                nc.vector.tensor_tensor(near, m[:, :, 1], m[:, :, 4], ALU.subtract)
                nc.vector.tensor_tensor(square, m[:, :, 2], m[:, :, 5], ALU.add)
                nc.vector.tensor_tensor(twice_mean, m[:, :, 1], m[:, :, 4], ALU.add).then_inc(sems[1], 1)
                dve.wait_ge(sems[1], s.at(1))
                nc.vector.scalar_tensor_tensor(near, near, 0.25, near, ALU.mult, ALU.mult).then_inc(sems[2], 1)
                dve.wait_ge(sems[2], s.at(1))
                nc.vector.scalar_tensor_tensor(into, square, 1.0 / D, near, ALU.mult, ALU.add).then_inc(sems[3], 1)

            def attend(s):
                b = s.back(1)
                if s.exists():
                    u = s.u
                    wait(dve, att.gathered[u], s.uses(1, BOTH_GATHERED))
                    wait(dve, att.endsT_done, s.at(-1))
                    nc.vector.scalar_tensor_tensor(ends_pre[:, u], ends[:, u, :, 0:D], SLOPE, ends[:, u, :, 0:D],
                                                   ALU.mult, ALU.max).then_inc(att.ends_leaky, 1)
                    wait(dve, att.ends_leaky, s.at(1))
                    nc.vector.tensor_tensor(ends_pre[:, u], ends_pre[:, u], ends[:, u, :, D:2 * D],
                                            ALU.add).then_inc(att.ends_made, 1)
                    dve.wait_ge(att.ends_made, s.at(1))
                    measure(ends_pre[:, u], moments[:, u], 0, 2 * TG, att.ends_measured)
                if b.exists():
                    wait(dve, att.q_copied, b.at(1))
                    for h in range(2):
                        kv = bank[3 + 2 * b.u + h][0:P, 0:4 * D].rearrange("p (j d) -> p j d", d=2 * D)
                        made = nc.vector.tensor_tensor(prod[:, 2 * h:2 * h + 2, :], q_sb[:, b.u, 2 * h:2 * h + 2, :],
                                                       kv[:, :, 0:D], ALU.mult)
                    made.then_inc(att.prod_made, 1)
                    dve.wait_ge(att.prod_made, b.at(1))
                    nc.vector.tensor_reduce(scores[:].rearrange("p j h -> p (j h)"),
                                            prod[:].rearrange("p j (h d) -> p (j h) d", d=DH), AX.X,
                                            ALU.add).then_inc(att.score_made, 1)
                    dve.wait_ge(att.score_made, b.at(1))
                    nc.vector.tensor_tensor(scores[:], scores[:], both_rstd[:, b.u, :, None].to_broadcast([P, TG, HEADS]),
                                            ALU.mult).then_inc(att.scaled_made, 1)
                    dve.wait_ge(att.scaled_made, b.at(1))
                    wait(dve, att.exp_made, b.at(0))
                    nc.vector.tensor_scalar(clipped[:], scores[:], -CLIP, CLIP, ALU.max, ALU.min).then_inc(att.clip_made, 1)
                if s.exists():
                    wait(dve, att.nodes_in[s.u], s.uses(1, NODE_DMAS))
                    wait(dve, att.x1_made, s.at(-1))
                    nc.vector.scalar_tensor_tensor(nodes_pre[:, s.u], nodes_zx[:, s.u, :, 0:D], SLOPE, nodes_zx[:, s.u, :, 0:D],
                                                   ALU.mult, ALU.max).then_inc(att.nodes_leaky, 1)
                    wait(dve, att.nodes_leaky, s.at(1))
                    nc.vector.tensor_tensor(nodes_pre[:, s.u], nodes_pre[:, s.u], nodes_zx[:, s.u, :, D:2 * D],
                                            ALU.add).then_inc(att.nodes_made, 1)
                    dve.wait_ge(att.nodes_made, s.at(1))
                    measure(nodes_pre[:, s.u], moments[:, s.u], 2 * TG, ROWS, att.nodes_measured)
                    variance(s, (att.nodes_measured, att.halves_added, att.spread_made, att.var_made),
                             moments[:, s.u], apart, squares, mean2[:, s.u, :], var[:, s.u, :])
                if b.exists():
                    wait(dve, att.src_in[b.u], b.uses(1, 16))
                    wait(dve, att.sums_done, b.at(0))
                    for j in range(TG):
                        compared = nc.vector.tensor_scalar(same[:, j, :], src_row[0:P, b.u, :],
                                                           src_f[:, bass.ds(b.value(TG, j), 1)], None, ALU.is_equal)
                    compared.then_inc(att.same_made, 1)
                    wait(dve, att.exp_made, b.at(1))
                    nc.vector.tensor_tensor(weight_rstd[:], vals[:, b.u, :, D:DV],
                                            rstd[:, b.u, TG:2 * TG, None].to_broadcast([P, TG, HEADS]),
                                            ALU.mult).then_inc(att.weight_made, 1)
                    dve.wait_ge(att.weight_made, b.at(1))
                    for j in range(TG):
                        v = bank[3 + 2 * b.u + j // 2][0:P, (j % 2) * 2 * D + D:(j % 2 + 1) * 2 * D]
                        made = nc.vector.tensor_tensor(
                            vals[:, b.u, j, 0:D].rearrange("p (h d) -> p h d", d=DH),
                            v.rearrange("p (h d) -> p h d", d=DH),
                            weight_rstd[:, j, :, None].to_broadcast([P, HEADS, DH]), ALU.mult)
                    made.then_inc(att.val_made, 1)
                if s.exists():
                    wait(dve, att.std_made, s.at(1))
                    nc.vector.reciprocal(rstd[:, s.u, :], std[:, s.u, :]).then_inc(att.rstd_made, 1)
                    dve.wait_ge(att.rstd_made, s.at(1))
                    nc.vector.tensor_tensor(both_rstd[:, s.u, :], rstd[:, s.u, 0:TG], rstd[:, s.u, TG:2 * TG],
                                            ALU.mult).then_inc(att.ends_scaled, 1)
                    nc.vector.scalar_tensor_tensor(shift[:, s.u, :], mean2[:, s.u, 2 * TG:], -0.5, rstd[:, s.u, 2 * TG:],
                                                   ALU.mult, ALU.mult).then_inc(att.shift_made, 1)

            for u in range(2):
                dve.wait_ge(layers[1].put_done[u], ALL_PUT)
            pipeline(dve, GROUPS, 1, attend)

            for u in range(2):
                dve.wait_ge(att.put_done[u], ALL_PUT)
            dve.wait_ge(att.x1_made, GROUPS)

            def finish(s):
                b = s.back(1)
                if s.exists():
                    wait(dve, last.blocks_in[s.u], s.uses(1, 2 * NODE_DMAS))
                    wait(dve, last.inv_made, s.at(0))
                    nc.vector.tensor_scalar(den[:], last_sums[:, s.u, :, D:DV], NORM_EPS, None, ALU.add).then_inc(last.den_made, 1)
                    dve.wait_ge(last.den_made, s.at(1))
                    wait(dve, last.res_made, s.at(-1))
                    nc.vector.reciprocal(inv_den[:, s.u], den[:].rearrange("p r h -> p (r h)")
                                         ).then_inc(last.inv_made, 1)
                if b.exists():
                    dve.wait_ge(last.pre_made, b.at(1))
                    measure(last_pre[:, b.u], last_moments[:, b.u], 0, LAST_ROWS, last.measured)
                    variance(b, (last.measured, last.halves_added, last.spread_made, last.var_made),
                             last_moments[:, b.u], last_apart, last_squares, last_mean2[:, b.u, :], last_var[:, b.u, :])
                    wait(dve, last.std_made, b.at(1))
                    nc.vector.reciprocal(last_rstd[:, b.u, :], last_std[:, b.u, :]).then_inc(last.rstd_made, 1)
                    dve.wait_ge(last.rstd_made, b.at(1))
                    nc.vector.scalar_tensor_tensor(last_shift[:, b.u, :], last_mean2[:, b.u, :], -0.5, last_rstd[:, b.u, :],
                                                   ALU.mult, ALU.mult).then_inc(last.shift_made, 1)
                if s.exists():
                    wait(dve, last.res_made, s.at(1))
                    wait(dve, last.out_made, s.at(-1))
                    nc.vector.scalar_tensor_tensor(last_pre[:, s.u], last_x1[:, s.u], 2.0, last_sums[:, s.u, :, 0:D],
                                                   ALU.mult, ALU.add).then_inc(last.pre_made, 1)

            pipeline(dve, LAST_BLOCKS, 1, finish)

        @block.tensor
        def _(pe):
            pe.wait_ge(loaded, 16 * OTHER_LOADS)
            pe.wait_ge(consts_made, 6)
            nc.tensor.matmul(bank[0][0:D, 0:3 * D], mean_of[:], wqkv[:], start=True, stop=True).then_inc(means_made, 1)
            for L in layers:
                n = L.n

                def take(s, L=L, n=n):
                    if n == 0:
                        wait(pe, L.nodes_in[s.u], s.uses(1, 16))
                        columns = x_cols[:, s.u, :].rearrange("d (p r) -> d r p", r=ROWS)
                    else:
                        wait(pe, L.nodes_leaky, s.at(1))
                        columns = nodeT[:, :, :].rearrange("d h (r p) -> d (h r) p", p=P)
                    for h in range(2 if n == 1 else 0):
                        wait(pe, L.nodeT_made[h], s.at(0))
                        for r in range(HALF):
                            done = nc.tensor.transpose(bank[4 + h][0:D, r * P:(r + 1) * P],
                                                       node_in[:, s.u, h * HALF + r, :], ident[0:P, 0:P])
                        done.then_inc(L.nodeT_done[h], 1)
                    for h in range(2):
                        if n == 1:
                            wait(pe, L.nodeT_made[h], s.at(1))
                        wait(pe, L.y_made[h], s.at(0))
                        for r in range(HALF):
                            done = nc.tensor.matmul(bank[6 + h][0:P, r * D:(r + 1) * D], columns[:, h * HALF + r, :],
                                                    wroot[n][:], start=True, stop=True)
                        done.then_inc(L.root_done[h], 1)

                pipeline(pe, GROUPS, 0, take)

                def put_steps(s, L=L, n=n):
                    b1, b2 = s.back(1), s.back(2)
                    if s.exists():
                        wait(pe, L.restaged, s.at(1))
                        wait(pe, L.featT_made, s.at(-1))
                        for j in range(TG):
                            done = nc.tensor.transpose(bank[s.u][:, j * P:(j + 1) * P], gath[:, s.u, j, :], ident[0:P, 0:P])
                        done.then_inc(L.feat_done, 1)
                    if b2.exists():
                        wait(pe, L.max_done, b2.at(1))
                        wait(pe, L.put_staged, b2.at(0))
                        for j in range(TG):
                            done = nc.tensor.transpose(bank[3][0:P, j * D:(j + 1) * D],
                                                       msg_max[:, b2.u, j * P:(j + 1) * P], ident[0:D, 0:D])
                        done.then_inc(L.back_done, 1)
                    if b1.exists():
                        wait(pe, L.featT_made, b1.at(1))
                        wait(pe, L.max_done, b1.at(0))
                        nc.tensor.matmul(bank[2][0:D, 0:GE], wcat[n][:], featT[:, b1.u, :], start=True,
                                         stop=True).then_inc(L.msg_done, 1)

                if n == 0:
                    pe.wait_ge(centered, 1)
                pipeline(pe, GROUPS, 2, put_steps)

            pe.wait_ge(layers[1].put_staged, GROUPS)

            def attend(s):
                b = s.back(1)
                if s.exists():
                    wait(pe, att.ends_made, s.at(1))
                    wait(pe, att.endsT_made, s.at(0))
                    for j in range(2 * TG):
                        done = nc.tensor.transpose(bank[j // TG][0:D, (j % TG) * P:(j % TG + 1) * P], ends_pre[:, s.u, j, :],
                                                   ident[0:P, 0:P])
                    done.then_inc(att.endsT_done, 1)
                    wait(pe, att.endsT_made, s.at(1))
                    wait(pe, att.q_copied, s.at(0))
                    wait(pe, att.val_made, s.at(-1))
                    for j in range(TG):
                        nc.tensor.matmul(bank[2][0:P, j * D:(j + 1) * D], endsT[0:D, 0, j * P:(j + 1) * P], wqkv[:, 0:D],
                                         start=True, stop=True)
                        done = nc.tensor.matmul(
                            bank[3 + 2 * s.u + j // 2][0:P, (j % 2) * 2 * D:(j % 2 + 1) * 2 * D],
                            endsT[0:D, 1, j * P:(j + 1) * P], wqkv[:, D:3 * D], start=True, stop=True)
                    done.then_inc(att.qkv_done, 1)
                if b.exists():
                    wait(pe, att.val_made, b.at(1))
                    wait(pe, att.sums_staged, b.at(0))
                    for t in range(TG):
                        for a in range(TG):
                            done = nc.tensor.matmul(bank[7][0:P, t * DV:(t + 1) * DV], same[:, a, t * P:(t + 1) * P],
                                                    vals[:, b.u, a, :], start=(a == 0), stop=(a == TG - 1))
                    done.then_inc(att.sums_done, 1)

            pipeline(pe, GROUPS, 1, attend)


def kernel(x, src, dst, edge_attr_32, L0_gnn_W1_msg, L0_gnn_W1_edge, L0_gnn_W1_root, L0_gnn_b1,
           L0_gnn_W2_msg, L0_gnn_W2_edge, L0_gnn_W2_root, L0_gnn_b2, L1_gnn_qW, L1_gnn_kW, L1_gnn_vW):
    import numpy as np
    import concourse.bacc as bacc
    from concourse.bass_utils import run_bass_kernel_spmd

    tile = 125
    src, dst = np.asarray(src), np.asarray(dst)
    arrays = {
        "x": x, "x_columns": np.asarray(x).T, "edge_attr": edge_attr_32,
        "src_tiles": src.reshape(-1, tile).T, "dst_tiles": dst.reshape(-1, tile).T,
        "dst_next_tiles": np.concatenate([dst[1:], np.full(1, -1, dst.dtype)]).reshape(-1, tile).T,
        "src_line": src,
        "dst_line": np.concatenate([dst[:1], dst]),
        "w1_msg": L0_gnn_W1_msg, "w2_msg": L0_gnn_W2_msg, "w1_edge": L0_gnn_W1_edge, "w2_edge": L0_gnn_W2_edge,
        "w1_root": L0_gnn_W1_root, "w2_root": L0_gnn_W2_root, "b1": L0_gnn_b1, "b2": L0_gnn_b2,
        "w_q": L1_gnn_qW, "w_k": L1_gnn_kW, "w_v": L1_gnn_vW,
    }
    nc = bacc.Bacc("TRN2", target_bir_lowering=False, num_devices=1)
    arrays = {k: np.ascontiguousarray(v) for k, v in arrays.items()}
    ap = {k: nc.dram_tensor(k, v.shape, mybir.dt.from_np(v.dtype), kind="ExternalInput").ap() for k, v in arrays.items()}
    out = nc.dram_tensor("out", arrays["x"].shape, F32, kind="ExternalOutput").ap()
    gnn_program(nc, ap["x"], ap["x_columns"], ap["edge_attr"], ap["src_tiles"], ap["dst_tiles"], ap["dst_next_tiles"],
                ap["src_line"], ap["dst_line"], (ap["w1_msg"], ap["w2_msg"]), (ap["w1_edge"], ap["w2_edge"]),
                (ap["w1_root"], ap["w2_root"]), (ap["b1"], ap["b2"]), ap["w_q"], ap["w_k"], ap["w_v"], out)
    r = run_bass_kernel_spmd(nc, [arrays], core_ids=[0])
    return r.results[0]["out"]
```
